# Optimizing a Trainium2 kernel written in Bass

```python
import numpy as np
import jax
import jax.numpy as jnp

def _softmax(x, axis=-1):
    return jax.nn.softmax(x, axis=axis)

def _gelu(x):
    return jax.nn.gelu(x, approximate=True)

def _silu(x):
    return jax.nn.silu(x)

def _sigmoid(x):
    return jax.nn.sigmoid(x)

def _layernorm(x, axis=-1, eps=1e-05):
    m = jnp.mean(x, axis=axis, keepdims=True)
    v = jnp.var(x, axis=axis, keepdims=True)
    return (x - m) / jnp.sqrt(v + eps)

def _scatter_add(tgt, idx, src, axis=0):
    return tgt.at[idx].add(src)

def _segment_sum(src, seg, n):
    return jax.ops.segment_sum(src, seg, n)
kernel_name = 'mk_adaln_d1_jaxref_r8_a389e4'

def setup_inputs(seed: int=0):
    np.random.seed(seed)
    _w = jnp.asarray

    def _L0_attn_setup():
        import jax, jax.numpy as jnp
        import numpy as np
        N_HEADS = 16
        WINDOW = 32

        def _sliding_window_bias(seq_len: int) -> jnp.ndarray:
            i = jnp.arange(seq_len)[:, None]
            j = jnp.arange(seq_len)[None, :]
            allowed = jnp.abs(i - j) <= WINDOW
            return jnp.where(allowed, 0.0, -jnp.inf).astype(jnp.float32)
        key = jax.random.key(seed)
        ks = jax.random.split(key, 6)
        B, S, D = (2, 256, 128)
        std = 0.02
        x = jax.random.normal(ks[0], (B, S, D), dtype=jnp.float32)
        wq = jax.random.normal(ks[1], (D, D), dtype=jnp.float32) * std
        wk = jax.random.normal(ks[2], (D, D), dtype=jnp.float32) * std
        wv = jax.random.normal(ks[3], (D, D), dtype=jnp.float32) * std
        wo = jax.random.normal(ks[4], (D, D), dtype=jnp.float32) * std
        bq = jnp.zeros((D,), jnp.float32)
        bk = jnp.zeros((D,), jnp.float32)
        bv = jnp.zeros((D,), jnp.float32)
        bo = jnp.zeros((D,), jnp.float32)
        return {'x': x, 'wq': wq, 'bq': bq, 'wk': wk, 'bk': bk, 'wv': wv, 'bv': bv, 'wo': wo, 'bo': bo}
    _L0_attn_in = _L0_attn_setup()

    def _L0_ffn_setup():
        import jax, jax.numpy as jnp
        import numpy as np
        DIM = 128
        HIDDEN = 128
        NUM_EXPERTS = 8
        TOP_K = 2
        key = jax.random.key(seed)
        ks = jax.random.split(key, 8)
        std = 0.02
        x = jax.random.normal(ks[0], (2, 128, DIM), dtype=jnp.float32)
        gate_w = jax.random.normal(ks[1], (NUM_EXPERTS, DIM), dtype=jnp.float32) * std
        w1 = jax.random.normal(ks[2], (NUM_EXPERTS, DIM, HIDDEN), dtype=jnp.float32) * std
        w2 = jax.random.normal(ks[3], (NUM_EXPERTS, HIDDEN, DIM), dtype=jnp.float32) * std
        w3 = jax.random.normal(ks[4], (NUM_EXPERTS, DIM, HIDDEN), dtype=jnp.float32) * std
        w1s = jax.random.normal(ks[5], (1, DIM, HIDDEN), dtype=jnp.float32) * std
        w2s = jax.random.normal(ks[6], (1, HIDDEN, DIM), dtype=jnp.float32) * std
        w3s = jax.random.normal(ks[7], (1, DIM, HIDDEN), dtype=jnp.float32) * std
        return {'x': x, 'gate_w': gate_w, 'w1': w1, 'w2': w2, 'w3': w3, 'w1s': w1s, 'w2s': w2s, 'w3s': w3s}
    _L0_ffn_in = _L0_ffn_setup()
    _L0_c = _w((lambda *s: np.random.randn(*s).astype(np.float32) * 0.05)(16, 128))
    _L0_wmod = _w((lambda *s: np.random.randn(*s).astype(np.float32) * 0.05)(128, 6 * 128) * 128 ** (-0.5))
    _d = {'L0_attn_x': _L0_attn_in['x'], 'L0_attn_wq': _L0_attn_in['wq'], 'L0_attn_bq': _L0_attn_in['bq'], 'L0_attn_wk': _L0_attn_in['wk'], 'L0_attn_bk': _L0_attn_in['bk'], 'L0_attn_wv': _L0_attn_in['wv'], 'L0_attn_bv': _L0_attn_in['bv'], 'L0_attn_wo': _L0_attn_in['wo'], 'L0_attn_bo': _L0_attn_in['bo'], 'L0_ffn_gate_w': _L0_ffn_in['gate_w'], 'L0_ffn_w1': _L0_ffn_in['w1'], 'L0_ffn_w2': _L0_ffn_in['w2'], 'L0_ffn_w3': _L0_ffn_in['w3'], 'L0_ffn_w1s': _L0_ffn_in['w1s'], 'L0_ffn_w2s': _L0_ffn_in['w2s'], 'L0_ffn_w3s': _L0_ffn_in['w3s'], 'L0_c': _L0_c, 'L0_wmod': _L0_wmod}
    _x0 = _d['L0_attn_x']
    _d['L0_attn_x'] = jax.random.normal(jax.random.fold_in(jax.random.key(seed), 1), (16, 512, 128), dtype=_x0.dtype)
    del _x0
    return _d

def reference(L0_attn_x, L0_attn_wq, L0_attn_bq, L0_attn_wk, L0_attn_bk, L0_attn_wv, L0_attn_bv, L0_attn_wo, L0_attn_bo, L0_ffn_gate_w, L0_ffn_w1, L0_ffn_w2, L0_ffn_w3, L0_ffn_w1s, L0_ffn_w2s, L0_ffn_w3s, L0_c, L0_wmod):

    def _L0_attn_ref(x, wq, bq, wk, bk, wv, bv, wo, bo):
        import jax, jax.numpy as jnp
        import numpy as np
        N_HEADS = 16
        WINDOW = 32

        def _sliding_window_bias(seq_len: int) -> jnp.ndarray:
            i = jnp.arange(seq_len)[:, None]
            j = jnp.arange(seq_len)[None, :]
            allowed = jnp.abs(i - j) <= WINDOW
            return jnp.where(allowed, 0.0, -jnp.inf).astype(jnp.float32)
        B, S, D = x.shape
        H = N_HEADS
        dh = D // H
        scale = dh ** (-0.5)
        q = (x @ wq.T + bq).reshape(B, S, H, dh).transpose(0, 2, 1, 3)
        k = (x @ wk.T + bk).reshape(B, S, H, dh).transpose(0, 2, 1, 3)
        v = (x @ wv.T + bv).reshape(B, S, H, dh).transpose(0, 2, 1, 3)
        scores = jnp.einsum('bhqd,bhkd->bhqk', q, k) * scale
        scores = scores + _sliding_window_bias(S)[None, None]
        attn = jax.nn.softmax(scores, axis=-1)
        out = jnp.einsum('bhqk,bhkd->bhqd', attn, v)
        out = out.transpose(0, 2, 1, 3).reshape(B, S, D)
        return out @ wo.T + bo

    def _L0_ffn_ref(x, gate_w, w1, w2, w3, w1s, w2s, w3s):
        import jax, jax.numpy as jnp
        import numpy as np
        DIM = 128
        HIDDEN = 128
        NUM_EXPERTS = 8
        TOP_K = 2
        bs, slen, dim = x.shape
        xt = x.reshape(bs * slen, dim)
        logits = xt @ gate_w.T
        scores = jax.nn.softmax(logits.astype(jnp.float32), axis=1).astype(x.dtype)
        top_scores, sel = jax.lax.top_k(scores, TOP_K)
        sel_flat = sel.reshape(-1)
        order = jnp.argsort(sel_flat, stable=True)
        top_scores_sorted = top_scores.reshape(-1)[order]
        token_idx = order // TOP_K
        eid = sel_flat[order]
        routed_in = xt[token_idx] * top_scores_sorted[:, None]
        out_routed = jnp.zeros_like(routed_in)
        for e in range(NUM_EXPERTS):
            m = (eid == e)[:, None]
            xe = jnp.where(m, routed_in, 0.0)
            h = jax.nn.silu(xe @ w1[e]) * (xe @ w3[e])
            out_routed = out_routed + jnp.where(m, h @ w2[e], 0.0)
        hs = jax.nn.silu(xt @ w1s[0]) * (xt @ w3s[0])
        out = hs @ w2s[0]
        out = out.at[token_idx].add(out_routed)
        return out.reshape(bs, slen, dim)
    x = L0_attn_x
    mod = (_silu(L0_c) @ L0_wmod).reshape(L0_c.shape[0], 6, 1, -1)
    sa, ca, ga, sb, cb, gb = (mod[:, 0], mod[:, 1], mod[:, 2], mod[:, 3], mod[:, 4], mod[:, 5])
    ga = (2 * (ga >= 0) - 1) * jnp.maximum(jnp.abs(ga), 0.25)
    gb = (2 * (gb >= 0) - 1) * jnp.maximum(jnp.abs(gb), 0.25)
    h = _layernorm(x, axis=-1) * (1 + ca) + sa
    x = x + ga * _L0_attn_ref(h, L0_attn_wq, L0_attn_bq, L0_attn_wk, L0_attn_bk, L0_attn_wv, L0_attn_bv, L0_attn_wo, L0_attn_bo)
    h = _layernorm(x, axis=-1) * (1 + cb) + sb
    x = x + gb * _L0_ffn_ref(h, L0_ffn_gate_w, L0_ffn_w1, L0_ffn_w2, L0_ffn_w3, L0_ffn_w1s, L0_ffn_w2s, L0_ffn_w3s)
    return x

_drawn_inputs = setup_inputs


def setup_inputs(seed=0):
    import zlib

    import numpy as np

    out = dict(_drawn_inputs(seed))
    spreads = {'L0_attn_bq': (0.0, 0.8),
     'L0_attn_bk': (0.0, 0.8),
     'L0_attn_bv': (0.0, 0.8),
     'L0_attn_bo': (0.0, 0.324)}
    factors = {'L0_attn_wq': 8.0,
     'L0_attn_wk': 8.0,
     'L0_attn_wv': 8.0,
     'L0_attn_wo': 8.0,
     'L0_ffn_gate_w': 8.0,
     'L0_ffn_w1': 8.0,
     'L0_ffn_w2': 8.0,
     'L0_ffn_w3': 8.0,
     'L0_ffn_w1s': 8.0,
     'L0_ffn_w2s': 8.0,
     'L0_ffn_w3s': 8.0}
    for name, (base, spread) in spreads.items():
        noise = np.random.default_rng([zlib.crc32(name.encode()), seed]).standard_normal(out[name].shape)
        drawn = base * np.exp(spread * noise) if base else spread * noise
        out[name] = jnp.asarray(drawn.astype(out[name].dtype))
    for name, factor in factors.items():
        out[name] = (out[name] * factor).astype(out[name].dtype)
    return out
```

```python
import numpy as np
import concourse.bass as bass
from concourse import mybir
from contextlib import ExitStack

F32 = mybir.dt.float32
F32R = mybir.dt.float32r
BF16 = mybir.dt.bfloat16
U32 = mybir.dt.uint32
ALU = mybir.AluOpType
ACT = mybir.ActivationFunctionType
AX = mybir.AxisListType

B, S, D = 16, 512, 128
H, DH = 16, 8
HG, HJ = 4, 4
WIN = 32
NE = 8
SCALE = DH ** -0.5
EPS = 1e-5
NEG = -1e30

QB = 128
QK = QB + 2 * WIN
NQB = S // QB
PB = 64
NPB = S // PB
SP_ = S + 2 * WIN
NMAX = NQB * H // 2
NSC = NPB * 2
NX = NE + 1
MROW = 24


def ln_sems(sem, name):
    return {k: sem(f"{name}_{k}") for k in ("mean", "xc", "sq", "var", "ve", "rstd", "nrm", "h", "hh", "hl")}


def build(nc, xT, w13, w2, wqkv, wo, gate, bias, cT, wmod, out):
    ctx = ExitStack()
    with ctx:
        def sb(name, shape, dt=F32):
            return ctx.enter_context(nc.sbuf_tensor(name, shape, dt))

        def sem(name):
            return ctx.enter_context(nc.semaphore(name))

        q_scr = nc.dram_tensor("q_scr", (HJ, 4, 32, S), F32, kind="Internal").ap()
        k_scr = nc.dram_tensor("k_scr", (HJ, 4, 32, S), F32, kind="Internal").ap()
        s_scr = nc.dram_tensor("s_scr", (NQB * NE, QB), F32, kind="Internal").ap()

        w13h = sb("w13h", [128, NX, 2, 128], F32R)
        w13l = sb("w13l", [128, NX, 2, 128], F32R)
        w2s = sb("w2s", [128, NX, 128])
        wqf = sb("wqf", [128, 3, 128])
        wqh = sb("wqh", [128, 3, 128], F32R)
        wql = sb("wql", [128, 3, 128], F32R)
        wof = sb("wof", [128, 128])
        wom = sb("wom", [128, HJ, 128])
        gw = sb("gw", [128, NE])
        bia = sb("bia", [128, 4])
        ct = sb("ct", [128, B])
        cth = sb("cth", [128, B])
        csl = sb("csl", [128, B])
        wm = sb("wm", [128, 6, 128])
        mod = sb("mod", [128, 6, B])
        mabs = sb("mabs", [128, 2, B])
        msgn = sb("msgn", [128, 2, B])
        gab = sb("gab", [128, 2, B])
        bo2 = sb("bo2", [128, 1])
        ident = sb("ident", [128, 128])
        identb = sb("identb", [128, 128], BF16)
        onesd = sb("onesd", [128, 128])
        ones = sb("ones", [128, 32])
        mhalf = sb("mhalf", [128, 1])
        zero = sb("zero", [128, 1])
        spare = sb("spare", [128, 1])
        fill = sb("fill", [128, 2, S])
        iota8 = sb("iota8", [128, NE])
        mq = sb("mq", [128, 3, QK], BF16)
        mk = sb("mk", [128, 3, PB], BF16)
        xt = sb("xt", [128, S])
        ln1 = {k: sb(f"l1_{k}", [128, S]) for k in ("xc", "sq", "ve", "rstd", "nrm", "h")}
        hhp = sb("hhp", [128, SP_], F32R)
        hlp = sb("hlp", [128, SP_], F32R)
        qf, kf = sb("qf", [128, S]), sb("kf", [128, S])
        qh, ql = sb("qh", [128, S], F32R), sb("ql", [128, S], F32R)
        kh, kl = sb("kh", [128, S], F32R), sb("kl", [128, S], F32R)
        v = sb("v", [128, NPB, 128])
        q4 = sb("q4", [128, HG, HJ, S], F32R)
        k4 = sb("k4", [128, HG, SP_], F32R)
        mx = sb("mx", [128, NQB, HJ, HG])
        mT = sb("mT", [H, S], F32R)
        p = sb("p", [128, 2, H * PB])
        rden = sb("rden", [128, HJ * PB])
        o = sb("o", [128, HJ, S])
        yt = sb("yt", [128, S])
        x2 = sb("x2", [128, S])
        ln2 = {k: sb(f"l2_{k}", [128, S]) for k in ("xc", "sq", "ve", "rstd", "nrm", "h")}
        h2h = sb("h2h", [128, S], F32R)
        h2l = sb("h2l", [128, S], F32R)
        rm, dl, ex = sb("rm", [128, NQB]), sb("dl", [128, NQB, NE]), sb("ex", [128, NQB, NE])
        es, er, sc = sb("es", [128, NQB]), sb("er", [128, NQB]), sb("sc", [128, NQB, NE])
        m8 = sb("m8", [128, NQB, 8])
        ix = sb("ix", [128, NQB, 8], U32)
        ixf = sb("ixf", [128, NQB, 2])
        sel = sb("sel", [128, 2, NQB, NE])
        selb = sb("selb", [128, NQB, NE])
        sm = sb("sm", [128, NQB, NE])
        smT = sb("smT", [NQB * NE, QB])
        sbc = sb("sbc", [128, NQB, NE, QB])
        land = sbc[:].rearrange("p a e n -> p (a e n)")
        w13f = land[:, 0:NX * 256].rearrange("p (e k n) -> p e k n", e=NX, k=2)
        w2f = land[:, NX * 256:NX * 384].rearrange("p (e n) -> p e n", e=NX)
        x2c = sb("x2c", [128, S])
        t, u = sb("t", [128, 2, S]), sb("u", [128, 2, S])
        th, w = sb("th", [128, 2, S]), sb("w", [128, 2, S])
        g = sb("g", [128, 2, S])
        ot = sb("ot", [128, S])

        ps = {n: ctx.enter_context(nc.psum_tensor(f"ps_{n}", [128, 512], F32))
              for n in ("S0", "S1", "PV", "A", "B", "Y", "M0", "M1")}
        sc_ps = (ps["S0"], ps["S1"])

        w_in = sem("w_in")
        e_in = sem("e_in")
        cst = sem("cst")
        z_in = sem("z_in")
        scr0 = sem("scr0")
        s_th, s_sl, s_mod, s_wom = sem("s_th"), sem("s_sl"), sem("s_mod"), sem("s_wom")
        s_wh, s_wl, s_w2, s_bo, s_md = sem("s_wh"), sem("s_wl"), sem("s_w2"), sem("s_bo"), sem("s_md")
        s_sv = sem("s_sv")
        l1, l2 = ln_sems(sem, "l1"), ln_sems(sem, "l2")
        x_in = sem("x_in")
        q_mm, k_mm, v_mm = sem("q_mm"), sem("k_mm"), sem("v_mm")
        q_f, k_f, v_ev = sem("q_f"), sem("k_f"), sem("v_ev")
        q_h, k_h, q_l, k_l = sem("q_h"), sem("k_h"), sem("q_l"), sem("k_l")
        scr_w, qk_in = sem("scr_w"), sem("qk_in")
        ms_mm, mx_rd, mt_mm, mt_cp, m_in = sem("ms_mm"), sem("mx_rd"), sem("mt_mm"), sem("mt_cp"), sem("m_in")
        sc_mm, exp_d, pv_mm, rden_d, o_d = sem("sc_mm"), sem("exp_d"), sem("pv_mm"), sem("rden_d"), sem("o_d")
        wo_mm, y_d, x2_d, x2c_d = sem("wo_mm"), sem("y_d"), sem("x2_d"), sem("x2c_d")
        g_mm, g_dl, g_ex, g_ch, sm_d = sem("g_mm"), sem("g_dl"), sem("g_ex"), sem("g_ch"), sem("sm_d")
        smt_mm, smt_cp, s_wr, s_in = sem("smt_mm"), sem("smt_cp"), sem("s_wr"), sem("s_in")
        a_mm, b_mm, t_d, u_d, th_d, w_d, g_d = (sem(n) for n in ("a_mm", "b_mm", "t_d", "u_d", "th_d", "w_d", "g_d"))
        y_mm, fin_d, out_d = sem("y_mm"), sem("fin_d"), sem("out_d")

        NG = 11

        block = ctx.enter_context(nc.Block())

        def pipeline(eng, body):
            body(0, True, False)
            with eng.Fori(1, B - 1) as i:
                body(i, False, False)
            body(B - 1, False, True)

        def col(tile, k, b):
            return tile[:, k, bass.ds(b, 1)]

        @block.sync
        def _(sp):
            sp.dma_start(wqf[:], wqkv).then_inc(w_in, 16)
            sp.dma_start(ct[:], cT).then_inc(w_in, 16)
            sp.dma_start(wm[:], wmod).then_inc(w_in, 16)
            sp.dma_start(bia[:], bias).then_inc(w_in, 16)
            sp.dma_start(gw[:], gate).then_inc(w_in, 16)
            sp.dma_start(wof[:], wo).then_inc(w_in, 16)

            def load_x(b):
                if not (isinstance(b, int) and b == 0):
                    sp.wait_ge(x2_d, b)
                sp.dma_start(xt[:], xT[bass.ds(b, 1)]).then_inc(x_in, 16)

            def regroup(b):
                sp.wait_ge(k_h, b + 1)
                sp.dma_start(k_scr[:, 0], kh[:].bitcast(F32)).then_inc(scr_w, 16)
                sp.dma_start(k_scr[:, 1], kh[:].bitcast(F32)).then_inc(scr_w, 16)
                sp.wait_ge(q_h, b + 1)
                sp.dma_start(q_scr[:, 0], qh[:].bitcast(F32)).then_inc(scr_w, 16)
                sp.dma_start(q_scr[:, 2], qh[:].bitcast(F32)).then_inc(scr_w, 16)
                sp.wait_ge(q_l, b + 1)
                sp.dma_start(q_scr[:, 1], ql[:].bitcast(F32)).then_inc(scr_w, 16)
                sp.wait_ge(k_l, b + 1)
                sp.dma_start(k_scr[:, 2], kl[:].bitcast(F32)).then_inc(scr_w, 16)
                sp.wait_ge(scr_w, 96 * b + 96)
                if isinstance(b, int) and b == 0:
                    sp.wait_ge(z_in, 2)
                    sp.wait_ge(scr0, 32)
                sp.dma_start(k4[:, :, WIN:WIN + S].bitcast(F32),
                             k_scr.rearrange("j c (d g) s -> (j c d) g s", g=HG)).then_inc(qk_in, 16)
                for j in range(HJ):
                    sp.dma_start(q4[32 * j:32 * j + 32, :, j, :].bitcast(F32),
                                 q_scr[j].rearrange("c (d g) s -> (c d) g s", g=HG)).then_inc(qk_in, 16)

            def put_max(b):
                sp.wait_ge(mt_cp, b + 1)
                for j in range(HJ):
                    r = 32 * j + MROW
                    sp.dma_start(q4[r:r + 1, :, j, :].bitcast(F32),
                                 mT[HG * j:HG * j + HG, :].bitcast(F32)).then_inc(m_in, 16)

            def spread_scores(b):
                sp.wait_ge(smt_cp, b + 1)
                sp.dma_start(s_scr, smT[:]).then_inc(s_wr, 16)
                sp.wait_ge(s_wr, 16 * b + 16)
                if isinstance(b, int) and b == 0:
                    sp.wait_ge(s_wl, 2)
                    sp.wait_ge(s_w2, 1)
                src = s_scr.rearrange("(o a) n -> o (a n)", o=1).to_broadcast([128, NQB * NE * QB])
                sp.dma_start(sbc[:].rearrange("p a e n -> p (a e n)"), src).then_inc(s_in, 16)

            def store(b):
                sp.wait_ge(fin_d, b + 1)
                sp.dma_start(out[bass.ds(b, 1)], ot[:]).then_inc(out_d, 16)

            load_x(0)
            sp.wait_ge(cst, CST_ALL)
            sp.dma_start(k_scr[:, 3], fill[:, 0, :]).then_inc(scr0, 16)
            sp.dma_start(q_scr[:, 3], fill[:, 1, :]).then_inc(scr0, 16)
            sp.wait_ge(z_in, 1)
            for h in range(H):
                sp.dma_start(wom[DH * h:DH * h + DH, h % HJ, :], wo[DH * h:DH * h + DH, :]).then_inc(s_wom, 16)
            sp.dma_start(w13f, w13).then_inc(e_in, 16)
            sp.dma_start(w2f, w2).then_inc(e_in, 16)
            regroup(0)

            def body(b, first, last):
                put_max(b)
                if not first:
                    store(b - 1)
                if not last:
                    load_x(b + 1)
                spread_scores(b)
                if not last:
                    regroup(b + 1)

            pipeline(sp, body)
            store(B - 1)
            sp.wait_ge(out_d, 16 * B)

        CST = [0]

        @block.gpsimd
        def _(pool):
            def const(ins):
                CST[0] += 1
                ins.then_inc(cst, 1)
                pool.wait_ge(cst, CST[0])

            def keep(tile, pattern, base, cm, op=ALU.is_ge, val=NEG):
                const(nc.gpsimd.affine_select(out=tile, in_=tile, compare_op=op, fill=val, base=base,
                                              pattern=pattern, channel_multiplier=cm))

            const(nc.gpsimd.memset(ident[:], 0.0))
            keep(ident[:], [[-1, 128]], 0, 1, ALU.not_equal, 1.0)
            const(nc.gpsimd.tensor_copy(identb[:], ident[:]))
            const(nc.gpsimd.memset(onesd[:], 1.0 / D))
            const(nc.gpsimd.memset(ones[:], 1.0))
            const(nc.gpsimd.memset(mhalf[:], -0.5))
            const(nc.gpsimd.memset(zero[:], 0.0))
            const(nc.gpsimd.memset(fill[:, 0, :], 1.0))
            const(nc.gpsimd.memset(fill[:, 1, :], 0.0))
            const(nc.gpsimd.iota(iota8[:], [[1, NE]], base=0, channel_multiplier=0,
                                 allow_small_or_imprecise_dtypes=True))
            const(nc.gpsimd.memset(mq[:], 0.0))
            const(nc.gpsimd.memset(mk[:], 0.0))
            for e in range(3):
                keep(mq[:, e, :], [[1, QK]], 0, -1)
                keep(mq[:, e, :], [[-1, QK]], 2 * WIN, 1)
                keep(mk[:, e, :], [[-1, PB]], 0, 1)
                keep(mk[:, e, :], [[1, PB]], 2 * WIN, -1)
            keep(mq[:, 0, :], [[1, QK]], -WIN, 0)
            keep(mk[:, 0, :], [[0, PB]], -WIN, 1)
            keep(mq[:, 2, :], [[-1, QK]], QK - WIN - 1, 0)
            keep(mk[:, 2, :], [[0, PB]], 128 - WIN - 1, -1)

            def norm(b, s, ln):
                pool.wait_ge(s["ve"], b + 1)
                nc.gpsimd.tensor_tensor(ln["rstd"][:], ln["ve"][:], mhalf[:].to_broadcast([128, S]), ALU.pow).then_inc(s["rstd"], 1)
                pool.wait_ge(s["rstd"], b + 1)
                nc.gpsimd.tensor_tensor(ln["nrm"][:], ln["xc"][:], ln["rstd"][:], ALU.mult).then_inc(s["nrm"], 1)

            def low_h1(b):
                pool.wait_ge(l1["hh"], b + 1)
                nc.gpsimd.tensor_tensor(hlp[:, WIN:WIN + S], ln1["h"][:], hhp[:, WIN:WIN + S].bitcast(F32),
                                        ALU.subtract).then_inc(l1["hl"], 1)

            def low_qk(b):
                pool.wait_ge(q_h, b + 1)
                nc.gpsimd.tensor_tensor(ql[:], qf[:], qh[:].bitcast(F32), ALU.subtract).then_inc(q_l, 1)
                pool.wait_ge(k_h, b + 1)
                nc.gpsimd.tensor_tensor(kl[:], kf[:], kh[:].bitcast(F32), ALU.subtract).then_inc(k_l, 1)

            def low_h2(b):
                pool.wait_ge(l2["hh"], b + 1)
                nc.gpsimd.tensor_tensor(h2l[:], ln2["h"][:], h2h[:].bitcast(F32), ALU.subtract).then_inc(l2["hl"], 1)

            def keep_x2(b, first):
                pool.wait_ge(x2_d, b + 1)
                if not first:
                    pool.wait_ge(fin_d, b)
                nc.gpsimd.tensor_tensor(x2c[:], x2[:], zero[:].to_broadcast([128, S]), ALU.add).then_inc(x2c_d, 1)

            def expert(b, n, first):
                pool.wait_ge(u_d, NX * b + n + 1)
                if n >= 2 or not first:
                    pool.wait_ge(g_d, NX * b + max(n - 1, 0))
                nc.gpsimd.tensor_tensor(w[:, n % 2], t[:, n % 2], u[:, n % 2], ALU.mult).then_inc(w_d, 1)

            def stage_a(b):
                norm(b, l1, ln1)
                low_h1(b)
                low_qk(b)

            stage_a(0)

            def body(b, first, last):
                if not first:
                    for n in range(CSPLIT, CSPLIT + 1):
                        expert(b - 1, n, False)
                    expert(b - 1, CSPLIT + 1, False)
                norm(b, l2, ln2)
                if not first:
                    for n in range(CSPLIT + 2, NX):
                        expert(b - 1, n, False)
                low_h2(b)
                keep_x2(b, first)
                if not last:
                    norm(b + 1, l1, ln1)
                    low_h1(b + 1)
                    low_qk(b + 1)
                for n in range(0, CSPLIT):
                    expert(b, n, first)

            pipeline(pool, body)
            for n in range(CSPLIT, NX):
                expert(B - 1, n, False)

        CST_END = CST[0]
        assert CST_END == CST_ALL

        @block.scalar
        def _(act):
            act.wait_ge(w_in, 96)
            nc.scalar.activation(cth[:], ct[:], ACT.Tanh, scale=0.5).then_inc(s_th, 1)
            nc.scalar.activation(wqh[:], wqf[:], ACT.Copy).then_inc(s_wh, 1)
            act.wait_ge(e_in, 32)
            nc.scalar.activation(w13h[:], w13f, ACT.Copy).then_inc(s_wh, 1)
            nc.scalar.activation(w2s[:], w2f, ACT.Copy, scale=0.5).then_inc(s_w2, 1)

            def square(b, s, ln):
                act.wait_ge(s["xc"], b + 1)
                nc.scalar.activation(ln["sq"][:], ln["xc"][:], ACT.Square).then_inc(s["sq"], 1)

            def high_h1(b, first):
                act.wait_ge(l1["h"], b + 1)
                if not first:
                    act.wait_ge(v_mm, 2 * b)
                nc.scalar.activation(hhp[:, WIN:WIN + S], ln1["h"][:], ACT.Copy).then_inc(l1["hh"], 1)

            def high_qk(b, first):
                if not first:
                    act.wait_ge(scr_w, 96 * b)
                act.wait_ge(q_f, b + 1)
                nc.scalar.activation(qh[:], qf[:], ACT.Copy).then_inc(q_h, 1)
                act.wait_ge(k_f, b + 1)
                nc.scalar.activation(kh[:], kf[:], ACT.Copy).then_inc(k_h, 1)

            def copy_v(b, first):
                if not first:
                    act.wait_ge(pv_mm, NPB * b)
                for half, bank in ((0, "PV"), (1, "M0")):
                    act.wait_ge(v_mm, 2 * b + half + 1)
                    nc.scalar.activation(v[:, 4 * half:4 * half + 4, :], ps[bank][:], ACT.Copy).then_inc(v_ev, 1)

            def maxima(b, first):
                act.wait_ge(mt_mm, b + 1)
                if not first:
                    act.wait_ge(m_in, 64 * b)
                nc.scalar.activation(mT[:], ps["M1"][0:H, :], ACT.Copy, scale=-1.0).then_inc(mt_cp, 1)

            def probabilities(b):
                for n in range(NSC):
                    blk, half = n // 2, n % 2
                    act.wait_ge(sc_mm, NSC * b + n + 1)
                    if blk >= 2:
                        act.wait_ge(pv_mm, NPB * b + blk - 1)
                    nc.scalar.activation(p[:, blk % 2, 512 * half:512 * half + 512], sc_ps[n % 2][:],
                                         ACT.Exp).then_inc(exp_d, 1)

            def high_h2(b, first):
                act.wait_ge(l2["h"], b + 1)
                if not first:
                    act.wait_ge(b_mm, NX * b)
                nc.scalar.activation(h2h[:], ln2["h"][:], ACT.Copy).then_inc(l2["hh"], 1)

            def router_exp(b):
                act.wait_ge(g_dl, b + 1)
                nc.scalar.activation(ex[:], dl[:], ACT.Exp).then_inc(g_ex, 1)

            def router_scores(b, first):
                act.wait_ge(smt_mm, b + 1)
                if not first:
                    act.wait_ge(s_wr, 16 * b)
                nc.scalar.activation(smT[:], ps["M1"][0:NQB * NE, 0:QB], ACT.Copy).then_inc(smt_cp, 1)

            def expert(b, n, first):
                act.wait_ge(t_d, NX * b + n + 1)
                if n >= 2 or not first:
                    act.wait_ge(g_d, NX * b + max(n - 1, 0))
                nc.scalar.activation(th[:, n % 2], t[:, n % 2], ACT.Tanh, scale=0.5).then_inc(th_d, 1)

            square(0, l1, ln1)
            high_h1(0, True)
            high_qk(0, True)
            copy_v(0, True)

            def body(b, first, last):
                maxima(b, first)
                if not first:
                    expert(b - 1, CSPLIT, False)
                probabilities(b)
                if not first:
                    expert(b - 1, CSPLIT + 1, False)
                square(b, l2, ln2)
                if not first:
                    expert(b - 1, CSPLIT + 2, False)
                    expert(b - 1, CSPLIT + 3, False)
                high_h2(b, first)
                if not last:
                    square(b + 1, l1, ln1)
                router_exp(b)
                router_scores(b, first)
                if not last:
                    high_h1(b + 1, False)
                    high_qk(b + 1, False)
                    copy_v(b + 1, False)
                for n in range(0, CSPLIT):
                    expert(b, n, first)

            pipeline(act, body)
            for n in range(CSPLIT, NX):
                expert(B - 1, n, False)

        @block.vector
        def _(dve):
            nc.vector.memset(wom[:], 0.0).then_inc(z_in, 1)
            nc.vector.memset(q4[:].bitcast(F32), 0.0)
            nc.vector.memset(k4[:].bitcast(F32), 0.0)
            nc.vector.memset(hhp[:].bitcast(F32), 0.0)
            nc.vector.memset(hlp[:].bitcast(F32), 0.0).then_inc(z_in, 1)
            dve.wait_ge(s_th, 1)
            nc.vector.scalar_tensor_tensor(cth[:], cth[:], 1.0, ct[:], ALU.add, ALU.mult).then_inc(s_sv, 1)
            dve.wait_ge(s_sv, 1)
            nc.vector.tensor_scalar(csl[:], cth[:], 0.5, None, ALU.mult).then_inc(s_sl, 1)
            dve.wait_ge(s_wh, 1)
            nc.vector.tensor_tensor(wql[:], wqf[:], wqh[:].bitcast(F32), ALU.subtract).then_inc(s_wl, 1)
            dve.wait_ge(s_mod, 1)
            pm = ps["M1"][:, 0:6 * B].rearrange("p (k b) -> p k b", k=6)
            nc.vector.tensor_copy(mod[:], pm).then_inc(s_sv, 1)
            dve.wait_ge(s_sv, 2)
            for k in (1, 4):
                nc.vector.tensor_scalar(mod[:, k, :], pm[:, k, :], 1.0, None, ALU.add)
            mg = mod[:, 2:6:3, :]
            nc.vector.tensor_scalar(mabs[:], mg, -1.0, None, ALU.mult).then_inc(s_sv, 1)
            nc.vector.tensor_scalar(msgn[:], mg, 0.0, 2.0, ALU.is_ge, ALU.mult).then_inc(s_sv, 1)
            dve.wait_ge(s_sv, 4)
            nc.vector.tensor_tensor(mabs[:], mabs[:], mg, ALU.max).then_inc(s_sv, 1)
            dve.wait_ge(s_sv, 5)
            nc.vector.tensor_scalar(mabs[:], mabs[:], 0.25, None, ALU.max).then_inc(s_sv, 1)
            dve.wait_ge(s_sv, 6)
            nc.vector.scalar_tensor_tensor(gab[:], msgn[:], -1.0, mabs[:], ALU.add, ALU.mult).then_inc(s_md, 1)
            dve.wait_ge(s_bo, 1)
            nc.vector.tensor_scalar(bo2[:], ps["Y"][:, 0:1], bia[:, 3:4], None, ALU.add).then_inc(s_md, 1)
            dve.wait_ge(s_md, 2)

            def centre(b, s, ln, src, bank):
                dve.wait_ge(s["mean"], b + 1)
                nc.vector.tensor_tensor(ln["xc"][:], src[:], ps[bank][:], ALU.subtract).then_inc(s["xc"], 1)

            def variance(b, s, ln, bank):
                dve.wait_ge(s["var"], b + 1)
                nc.vector.tensor_scalar(ln["ve"][:], ps[bank][:], EPS, None, ALU.add).then_inc(s["ve"], 1)

            def modulate(b, s, ln, k, first):
                dve.wait_ge(s["nrm"], b + 1)
                if not first:
                    dve.wait_ge(s["hl"], b)
                nc.vector.tensor_scalar(ln["h"][:], ln["nrm"][:], col(mod, k + 1, b), col(mod, k, b),
                                        ALU.mult, ALU.add).then_inc(s["h"], 1)

            def bias_qk(b, first):
                dve.wait_ge(q_mm, b + 1)
                if not first:
                    dve.wait_ge(q_l, b)
                nc.vector.tensor_scalar(qf[:], ps["S0"][:], bia[:, 0:1], SCALE, ALU.add, ALU.mult).then_inc(q_f, 1)
                dve.wait_ge(k_mm, b + 1)
                if not first:
                    dve.wait_ge(k_l, b)
                nc.vector.tensor_scalar(kf[:], ps["S1"][:], bia[:, 1:2], None, ALU.add).then_inc(k_f, 1)

            def maxima(b, first):
                if not first:
                    dve.wait_ge(mt_mm, b)
                for n in range(NMAX):
                    qb, hp = n // (H // 2), n % (H // 2)
                    gg, j0 = hp // 2, 2 * (hp % 2)
                    dve.wait_ge(ms_mm, NMAX * b + n + 1)
                    nc.vector.tensor_reduce(mx[:, qb, j0:j0 + 2, gg],
                                            sc_ps[n % 2][:, 0:2 * QK].rearrange("p (a k) -> p a k", a=2),
                                            AX.X, ALU.max).then_inc(mx_rd, 1)

            def normalise(b, first):
                if not first:
                    dve.wait_ge(wo_mm, b)
                for blk in range(NPB):
                    dve.wait_ge(pv_mm, NPB * b + blk + 1)
                    nc.vector.reciprocal(rden[:], ps["PV"][:, 256:512]).then_inc(rden_d, 1)
                    dve.wait_ge(rden_d, NPB * b + blk + 1)
                    nc.vector.tensor_tensor(o[:, :, PB * blk:PB * blk + PB],
                                            ps["PV"][:, 0:256].rearrange("p (j q) -> p j q", j=HJ),
                                            rden[:].rearrange("p (j q) -> p j q", j=HJ), ALU.mult).then_inc(o_d, 1)

            def residual(b, first):
                dve.wait_ge(wo_mm, b + 1)
                nc.vector.tensor_scalar(yt[:], ps["M1"][:], bo2[:, 0:1], col(gab, 0, b),
                                        ALU.add, ALU.mult).then_inc(y_d, 1)
                dve.wait_ge(y_d, b + 1)
                if not first:
                    dve.wait_ge(x2c_d, b)
                nc.vector.tensor_tensor(x2[:], yt[:], xt[:], ALU.add).then_inc(x2_d, 1)

            def router(b):
                done = [0]

                def link(ins):
                    done[0] += 1
                    ins.then_inc(g_ch, 1)
                    dve.wait_ge(g_ch, NG * b + done[0])

                lg = ps["M1"][:, 0:NQB * NE].rearrange("p (a e) -> p a e", a=NQB)
                bc = [128, NQB, NE]
                dve.wait_ge(g_mm, b + 1)
                link(nc.vector.tensor_reduce(rm[:], lg, AX.X, ALU.max))
                nc.vector.tensor_tensor(dl[:], lg, rm[:].unsqueeze(2).to_broadcast(bc), ALU.subtract).then_inc(g_dl, 1)
                dve.wait_ge(g_ex, b + 1)
                link(nc.vector.tensor_reduce(es[:], ex[:], AX.X, ALU.add))
                link(nc.vector.reciprocal(er[:], es[:]))
                link(nc.vector.tensor_tensor(sc[:], ex[:], er[:].unsqueeze(2).to_broadcast(bc), ALU.mult))
                nc.vector.memset(spare[:], 0.0)
                for a in range(NQB):
                    last = nc.vector.max(m8[:, a, :], sc[:, a, :])
                link(last)
                nc.vector.memset(spare[:], 0.0)
                for a in range(NQB):
                    last = nc.vector.max_index(ix[:, a, :], m8[:, a, :], sc[:, a, :])
                link(last)
                link(nc.vector.tensor_copy(ixf[:], ix[:, :, 0:2]))
                for r in range(2):
                    link(nc.vector.tensor_tensor(sel[:, r], iota8[:].unsqueeze(1).to_broadcast(bc),
                                                 ixf[:, :, r:r + 1].to_broadcast(bc), ALU.is_equal))
                link(nc.vector.tensor_tensor(selb[:], sel[:, 0], sel[:, 1], ALU.add))
                nc.vector.tensor_tensor(sm[:], sc[:], selb[:], ALU.mult).then_inc(g_ch, 1)
                assert done[0] + 1 == NG

            def gate_w(b, n, dst, bank, buf):
                if n == 0:
                    return nc.vector.tensor_copy(dst[:, buf], ps[bank][:])
                return nc.vector.tensor_tensor(dst[:, buf].rearrange("p (a n) -> p a n", a=NQB),
                                               ps[bank][:].rearrange("p (a n) -> p a n", a=NQB),
                                               sbc[:, :, n - 1, :], ALU.mult)

            def combine(b, n, first):
                dve.wait_ge(th_d, NX * b + n + 1)
                dve.wait_ge(w_d, NX * b + n + 1)
                if n >= 2 or not first:
                    dve.wait_ge(y_mm, NX * b + max(n - 1, 0))
                nc.vector.scalar_tensor_tensor(g[:, n % 2], th[:, n % 2], 1.0, w[:, n % 2],
                                               ALU.add, ALU.mult).then_inc(g_d, 1)

            def expert(b, n, first):
                dve.wait_ge(a_mm, NX * b + n + 1)
                if n == 1:
                    dve.wait_ge(s_in, 16 * b + 16)
                if n >= 2 or not first:
                    dve.wait_ge(w_d, NX * b + max(n - 1, 0))
                    dve.wait_ge(th_d, NX * b + max(n - 1, 0))
                gate_w(b, n, t, "A", n % 2).then_inc(t_d, 1)
                dve.wait_ge(b_mm, NX * b + n + 1)
                gate_w(b, n, u, "B", n % 2).then_inc(u_d, 1)
                if n >= 1:
                    combine(b, n - 1, first)

            def finish(b, first):
                combine(b, NX - 1, False)
                dve.wait_ge(y_mm, NX * b + NX)
                dve.wait_ge(x2c_d, b + 1)
                if not first:
                    dve.wait_ge(out_d, 16 * b)
                nc.vector.scalar_tensor_tensor(ot[:], ps["Y"][:], col(gab, 1, b), x2c[:],
                                               ALU.mult, ALU.add).then_inc(fin_d, 1)

            def split_experts():
                dve.wait_ge(s_wh, 2)
                nc.vector.tensor_tensor(w13l[:], w13f, w13h[:].bitcast(F32), ALU.subtract).then_inc(s_wl, 1)

            centre(0, l1, ln1, xt, "M0")
            variance(0, l1, ln1, "M0")
            modulate(0, l1, ln1, 0, True)
            bias_qk(0, True)
            split_experts()

            def body(b, first, last):
                maxima(b, first)
                if not first:
                    expert(b - 1, CSPLIT, False)
                normalise(b, first)
                residual(b, first)
                centre(b, l2, ln2, x2, "M1")
                if not first:
                    expert(b - 1, CSPLIT + 1, False)
                variance(b, l2, ln2, "M1")
                if not first:
                    expert(b - 1, CSPLIT + 2, False)
                    expert(b - 1, CSPLIT + 3, False)
                    finish(b - 1, first)
                modulate(b, l2, ln2, 3, first)
                if not last:
                    centre(b + 1, l1, ln1, xt, "M0")
                router(b)
                if not last:
                    variance(b + 1, l1, ln1, "M0")
                    modulate(b + 1, l1, ln1, 0, False)
                    bias_qk(b + 1, False)
                for n in range(0, CSPLIT):
                    expert(b, n, first)

            pipeline(dve, body)
            for n in range(CSPLIT, NX):
                expert(B - 1, n, False)
            finish(B - 1, False)

        @block.tensor
        def _(pe):
            mm = nc.tensor.matmul

            def exact3(dst, wh, wl, xh, xl):
                mm(dst, wh, xh, start=True, stop=False)
                mm(dst, wl, xh, start=False, stop=False)
                return mm(dst, wh, xl, start=False, stop=True)

            pe.wait_ge(w_in, 96)
            pe.wait_ge(cst, CST_ALL)
            pe.wait_ge(s_sl, 1)
            for k in range(6):
                last = mm(ps["M1"][:, k * B:k * B + B], wm[:, k, :], csl[:], start=True, stop=True)
            last.then_inc(s_mod, 1)
            mm(ps["Y"][:, 0:1], wof[:], bia[:, 2:3], start=True, stop=True).then_inc(s_bo, 1)

            def mean(b, s, src, ready, count, bank):
                pe.wait_ge(ready, count)
                mm(ps[bank][:], onesd[:], src[:], start=True, stop=True).then_inc(s["mean"], 1)

            def var(b, s, ln, bank):
                pe.wait_ge(s["sq"], b + 1)
                mm(ps[bank][:], onesd[:], ln["sq"][:], start=True, stop=True).then_inc(s["var"], 1)

            def project(b, first):
                pe.wait_ge(l1["hl"], b + 1)
                if not first:
                    pe.wait_ge(exp_d, NSC * b)
                    pe.wait_ge(o_d, NPB * b)
                hh, hl = hhp[:, WIN:WIN + S], hlp[:, WIN:WIN + S]
                exact3(ps["S0"][:], wqh[:, 0, :], wql[:, 0, :], hh, hl).then_inc(q_mm, 1)
                exact3(ps["S1"][:], wqh[:, 1, :], wql[:, 1, :], hh, hl).then_inc(k_mm, 1)
                for half, bank in ((0, "PV"), (1, "M0")):
                    for i in range(4):
                        win = slice(PB * (4 * half + i), PB * (4 * half + i) + 128)
                        dst = ps[bank][:, 128 * i:128 * i + 128]
                        mm(dst, hhp[:, win], wqh[:, 2, :], start=True, stop=False)
                        mm(dst, hhp[:, win], wql[:, 2, :], start=False, stop=False)
                        last = mm(dst, hlp[:, win], wqh[:, 2, :], start=False, stop=True)
                    last.then_inc(v_mm, 1)

            def maxima(b, first):
                pe.wait_ge(qk_in, 80 * b + 80)
                for n in range(NMAX):
                    qb, hp = n // (H // 2), n % (H // 2)
                    gg, j0 = hp // 2, 2 * (hp % 2)
                    edge = 0 if qb == 0 else 2 if qb == NQB - 1 else 1
                    if n >= 2:
                        pe.wait_ge(mx_rd, NMAX * b + n - 1)
                    bank = sc_ps[n % 2]
                    mm(bank[:, 0:2 * QK], identb[:], mq[:, edge, :].unsqueeze(1).to_broadcast([128, 2, QK]),
                       start=True, stop=False)
                    for a in range(2):
                        last = mm(bank[:, QK * a:QK * a + QK], q4[:, gg, j0 + a, QB * qb:QB * qb + QB],
                                  k4[:, gg, QB * qb:QB * qb + QK], start=False, stop=a == 1)
                    last.then_inc(ms_mm, 1)
                pe.wait_ge(mx_rd, NMAX * b + NMAX)
                if not first:
                    pe.wait_ge(smt_cp, b)
                for qb in range(NQB):
                    last = nc.tensor.transpose(ps["M1"][0:H, QB * qb:QB * qb + QB],
                                               mx[:, qb].rearrange("p j g -> p (j g)"), ident[:])
                last.then_inc(mt_mm, 1)

            def values(b, blk):
                pe.wait_ge(exp_d, NSC * b + 2 * blk + 2)
                if blk == 0:
                    pe.wait_ge(v_ev, 2 * b + 2)
                else:
                    pe.wait_ge(o_d, NPB * b + blk)
                for c in range(HG):
                    r = slice(32 * c, 32 * c + 32)
                    mm(ps["PV"][r, 0:256], v[:, blk, r], p[:, blk % 2, 256 * c:256 * c + 256], start=True, stop=True)
                for c in range(HG):
                    r = slice(32 * c, 32 * c + 32)
                    last = mm(ps["PV"][r, 256:512], ones[:], p[:, blk % 2, 256 * c:256 * c + 256],
                              start=True, stop=True)
                last.then_inc(pv_mm, 1)

            def scores(b):
                pe.wait_ge(m_in, 64 * b + 64)
                for blk in range(NPB):
                    edge = 0 if blk == 0 else 2 if blk == NPB - 1 else 1
                    for half in range(2):
                        n = 2 * blk + half
                        if n >= 2:
                            pe.wait_ge(exp_d, NSC * b + n - 1)
                        bank = sc_ps[n % 2]
                        mm(bank[:], identb[:], mk[:, edge, :].unsqueeze(1).to_broadcast([128, 8, PB]),
                           start=True, stop=False)
                        for a in range(2):
                            gg = 2 * half + a
                            last = mm(bank[:, 256 * a:256 * a + 256], k4[:, gg, PB * blk:PB * blk + 128],
                                      q4[:, gg, :, PB * blk:PB * blk + PB], start=False, stop=a == 1)
                        last.then_inc(sc_mm, 1)
                    if blk >= 1:
                        values(b, blk - 1)
                values(b, NPB - 1)

            def attn_out(b):
                pe.wait_ge(o_d, NPB * b + NPB)
                for j in range(HJ):
                    last = mm(ps["M1"][:], wom[:, j, :], o[:, j, :], start=j == 0, stop=j == HJ - 1)
                last.then_inc(wo_mm, 1)

            def router(b):
                pe.wait_ge(l2["h"], b + 1)
                for a in range(NQB):
                    last = mm(ps["M1"][:, NE * a:NE * a + NE], ln2["h"][:, QB * a:QB * a + QB], gw[:],
                              start=True, stop=True)
                last.then_inc(g_mm, 1)

            def router_t(b):
                pe.wait_ge(g_ch, NG * b + NG)
                nc.tensor.transpose(ps["M1"][0:NQB * NE, 0:QB], sm[:].rearrange("p a e -> p (a e)"),
                                    ident[:]).then_inc(smt_mm, 1)

            def down(b, n, first):
                pe.wait_ge(g_d, NX * b + n + 1)
                if n == 0 and not first:
                    pe.wait_ge(fin_d, b)
                e = (n - 1) % NX
                mm(ps["Y"][:], w2s[:, e, :], g[:, n % 2], start=n == 0, stop=n == NX - 1,
                   skip_group_check=False).then_inc(y_mm, 1)

            def expert(b, n, first):
                e = (n - 1) % NX
                if n == 0:
                    pe.wait_ge(l2["hl"], b + 1)
                if n >= 1 or not first:
                    pe.wait_ge(t_d, NX * b + n)
                exact3(ps["A"][:], w13h[:, e, 0, :], w13l[:, e, 0, :], h2h[:], h2l[:]).then_inc(a_mm, 1)
                if n >= 1 or not first:
                    pe.wait_ge(u_d, NX * b + n)
                exact3(ps["B"][:], w13h[:, e, 1, :], w13l[:, e, 1, :], h2h[:], h2l[:]).then_inc(b_mm, 1)
                if n >= 1:
                    down(b, n - 1, first)

            mean(0, l1, xt, x_in, 16, "M0")
            var(0, l1, ln1, "M0")
            pe.wait_ge(s_wl, 1)
            pe.wait_ge(z_in, 2)
            project(0, True)
            pe.wait_ge(s_wom, 16 * H)
            pe.wait_ge(s_md, 2)

            def body(b, first, last):
                maxima(b, first)
                if not first:
                    expert(b - 1, CSPLIT, False)
                scores(b)
                attn_out(b)
                mean(b, l2, x2, x2_d, b + 1, "M1")
                if not first:
                    expert(b - 1, CSPLIT + 1, False)
                var(b, l2, ln2, "M1")
                if not first:
                    expert(b - 1, CSPLIT + 2, False)
                    expert(b - 1, CSPLIT + 3, False)
                    down(b - 1, NX - 1, False)
                if not last:
                    mean(b + 1, l1, xt, x_in, 16 * b + 32, "M0")
                router(b)
                if not last:
                    var(b + 1, l1, ln1, "M0")
                router_t(b)
                if not last:
                    project(b + 1, False)
                if first:
                    pe.wait_ge(s_wl, 2)
                    pe.wait_ge(s_w2, 1)
                for n in range(0, CSPLIT):
                    expert(b, n, first)

            pipeline(pe, body)
            for n in range(CSPLIT, NX):
                expert(B - 1, n, False)
            down(B - 1, NX - 1, False)


CSPLIT = 5
CST_ALL = 28


def kernel(**inputs):
    import concourse.bacc as bacc
    from concourse.bass_utils import run_bass_kernel_spmd

    a = {k: np.asarray(x) for k, x in inputs.items()}
    order = np.arange(D).reshape(HG, HJ, DH).transpose(1, 2, 0).reshape(-1)
    lay = {
        "xT": a["L0_attn_x"].transpose(0, 2, 1),
        "w13": np.stack([np.concatenate([a["L0_ffn_w1"], a["L0_ffn_w1s"]]),
                         np.concatenate([a["L0_ffn_w3"], a["L0_ffn_w3s"]])]).transpose(2, 1, 0, 3),
        "w2": np.concatenate([a["L0_ffn_w2"], a["L0_ffn_w2s"]]).transpose(1, 0, 2),
        "wqkv": np.stack([a["L0_attn_wq"][order], a["L0_attn_wk"][order], a["L0_attn_wv"]]).transpose(2, 0, 1),
        "wo": a["L0_attn_wo"].T,
        "gate": a["L0_ffn_gate_w"].T,
        "bias": np.stack([a["L0_attn_bq"][order], a["L0_attn_bk"][order], a["L0_attn_bv"], a["L0_attn_bo"]]).T,
        "cT": a["L0_c"].T,
        "wmod": a["L0_wmod"].reshape(D, 6, D),
    }
    nc = bacc.Bacc("TRN2", target_bir_lowering=False, num_devices=1)
    arrays, args = {}, []
    for name, x in lay.items():
        arrays[name] = np.ascontiguousarray(x)
        args.append(nc.dram_tensor(name, x.shape, F32, kind="ExternalInput").ap())
    args.append(nc.dram_tensor("outT", (B, D, S), F32, kind="ExternalOutput").ap())
    build(nc, *args)
    r = run_bass_kernel_spmd(nc, [arrays], core_ids=[0])
    return np.ascontiguousarray(r.results[0]["outT"].transpose(0, 2, 1))
```

```python
import numpy as np
import concourse.bass as bass
from concourse import mybir
from contextlib import ExitStack

F32 = mybir.dt.float32
F32R = mybir.dt.float32r
BF16 = mybir.dt.bfloat16
U32 = mybir.dt.uint32
ALU = mybir.AluOpType
ACT = mybir.ActivationFunctionType
AX = mybir.AxisListType

B, S, D = 16, 512, 128
H, DH = 16, 8
HG, HJ = 4, 4
WIN = 32
NE = 8
SCALE = DH ** -0.5
EPS = 1e-5
NEG = -1e30

QB = 128
NQB = S // QB
MB = 32
MK = MB + 2 * WIN
NMB = S // MB
PB = 64
NPB = S // PB
SP_ = S + 2 * WIN
NSC = NPB * 2
NX = NE + 1
MROW = 24


def ln_sems(sem, name):
    return {k: sem(f"{name}_{k}") for k in ("bn", "ve", "rstd", "xn", "tr", "h", "hh", "hl")}


def build(nc, x, w13, w2, wqkv, wo, gate, bias, borow, cT, wmod, out):
    ctx = ExitStack()
    with ctx:
        def sb(name, shape, dt=F32):
            return ctx.enter_context(nc.sbuf_tensor(name, shape, dt))

        def sem(name):
            return ctx.enter_context(nc.semaphore(name))

        q_scr = nc.dram_tensor("q_scr", (HJ, 4, 32, S), F32, kind="Internal").ap()
        k_scr = nc.dram_tensor("k_scr", (HJ, 4, 32, S), F32, kind="Internal").ap()
        m_scr = nc.dram_tensor("m_scr", (B, 3, D), F32, kind="Internal").ap()
        s_scr = nc.dram_tensor("s_scr", (NQB * NE, QB), F32, kind="Internal").ap()

        w13h = sb("w13h", [128, NX, 2, 128], F32R)
        w13l = sb("w13l", [128, NX, 2, 128], F32R)
        w2s = sb("w2s", [128, NX, 128])
        wqh = sb("wqh", [128, 3, 128], F32R)
        wql = sb("wql", [128, 3, 128], F32R)
        wom = sb("wom", [128, HJ, 128])
        gw = sb("gw", [128, NE])
        bia = sb("bia", [128, 4])
        ct = sb("ct", [128, B])
        cth = sb("cth", [128, B])
        csl = sb("csl", [128, B])
        mod = sb("mod", [128, 4, B])
        mrow = sb("mrow", [B, 3, D])
        mall = sb("mall", [128, B, 3, D])
        ident = sb("ident", [128, 128])
        identb = sb("identb", [128, 128], BF16)
        dsel = sb("dsel", [128, NPB, 32])
        rsel = sb("rsel", [128, NPB, 128], F32R)
        mhalf = sb("mhalf", [128, 1])
        zero = sb("zero", [128, 1])
        spare = sb("spare", [128, 1])
        iota8 = sb("iota8", [128, NE])
        mq = sb("mq", [128, 3, MK], BF16)
        mk = sb("mk", [128, 3, PB], BF16)
        xt = sb("xt", [128, NQB, D])
        xb = sb("xb", [128, NQB, D])

        def ln_tiles(name):
            return {"st": sb(name + "_st", [128, NQB, 6]), "mv": sb(name + "_mv", [128, NQB, 2]),
                    "ve": sb(name + "_ve", [128, NQB]), "rstd": sb(name + "_rstd", [128, NQB]),
                    "xn": sb(name + "_xn", [128, NQB, D]), "h": sb(name + "_h", [128, S])}

        ln1, ln2 = ln_tiles("l1"), ln_tiles("l2")
        hhp = sb("hhp", [128, SP_], F32R)
        hlp = sb("hlp", [128, SP_], F32R)
        qf, kf = sb("qf", [128, S]), sb("kf", [128, S])
        qh, ql = sb("qh", [128, S], F32R), sb("ql", [128, S], F32R)
        kh, kl = sb("kh", [128, S], F32R), sb("kl", [128, S], F32R)
        v = sb("v", [128, NPB, 128])
        q4 = sb("q4", [128, HG, HJ, S], F32R)
        k4 = sb("k4", [128, HG, SP_], F32R)
        mx = sb("mx", [128, HG, NMB])
        mn = sb("mn", [128, HG, NMB], F32R)
        p = sb("p", [128, 2, H * PB])
        nm = sb("nm", [128, NPB, HJ, PB])
        rden = sb("rden", [128, HJ * PB])
        rdh, rdl = sb("rdh", [128, HJ * PB], F32R), sb("rdl", [128, HJ * PB], F32R)
        o = sb("o", [128, HJ, S])
        yt = sb("yt", [128, NQB, D])
        x2 = sb("x2", [128, NQB, D])
        h2h = sb("h2h", [128, S], F32R)
        h2l = sb("h2l", [128, S], F32R)
        rm, dl, ex = sb("rm", [128, NQB]), sb("dl", [128, NQB, NE]), sb("ex", [128, NQB, NE])
        es, er, sc = sb("es", [128, NQB]), sb("er", [128, NQB]), sb("sc", [128, NQB, NE])
        m8 = sb("m8", [128, NQB, 8])
        ix = sb("ix", [128, NQB, 8], U32)
        ixf = sb("ixf", [128, NQB, 2])
        sel = sb("sel", [128, 2, NQB, NE])
        selb = sb("selb", [128, NQB, NE])
        sm = sb("sm", [128, NE, NQB])
        smT = sb("smT", [NQB * NE, QB])
        sbc = sb("sbc", [128, NE, S])
        start_o = o[:].rearrange("p j s -> p (j s)")
        wm = start_o[:, 0:6 * D].rearrange("p (k d) -> p k d", k=6)
        wqf = start_o[:, 6 * D:9 * D].rearrange("p (k d) -> p k d", k=3)
        wof = start_o[:, 9 * D:10 * D]
        start_n = nm[0:B].rearrange("p k j q -> p (k j q)")
        mraw, mneg, mabs, msgn = (start_n[:, 2 * D * i:2 * D * i + 2 * D].rearrange("p (k d) -> p k d", k=2)
                                  for i in range(4))
        bob, bo2 = start_n[:, 8 * D:9 * D], start_n[:, 9 * D:10 * D]
        land = sbc[:].rearrange("p e s -> p (e s)")
        w13f = land[:, 0:NX * 256].rearrange("p (e k n) -> p e k n", e=NX, k=2)
        w2f = land[:, NX * 256:NX * 384].rearrange("p (e n) -> p e n", e=NX)
        x2c = sb("x2c", [128, NQB, D])
        t, u = sb("t", [128, 2, S]), sb("u", [128, 2, S])
        th = sb("th", [128, 2, S])
        g = sb("g", [128, 2, S])
        ot = sb("ot", [128, NQB, D])

        ps = {n: ctx.enter_context(nc.psum_tensor(f"ps_{n}", [128, 512], F32))
              for n in ("S0", "S1", "PV", "A", "B", "Y", "M0", "M1")}
        sc_ps = (ps["S0"], ps["S1"])
        mx_ps = (ps["S0"], ps["S1"], ps["PV"], ps["M0"])

        w_in = sem("w_in")
        e_in = sem("e_in")
        cst = sem("cst")
        cst_all = sem("cst_all")
        z_in = sem("z_in")
        scr0 = sem("scr0")
        s_th, s_sl, s_mod, s_wom = sem("s_th"), sem("s_sl"), sem("s_mod"), sem("s_wom")
        s_wh, s_wl, s_w2, s_bo, s_md = sem("s_wh"), sem("s_wl"), sem("s_w2"), sem("s_bo"), sem("s_md")
        s_sv, s_mr, s_mw, s_ma = sem("s_sv"), sem("s_mr"), sem("s_mw"), sem("s_ma")
        l1, l2 = ln_sems(sem, "l1"), ln_sems(sem, "l2")
        x_in = sem("x_in")
        q_mm, k_mm, v_mm = sem("q_mm"), sem("k_mm"), sem("v_mm")
        q_f, k_f, v_ev = sem("q_f"), sem("k_f"), sem("v_ev")
        q_h, k_h, q_l, k_l = sem("q_h"), sem("k_h"), sem("q_l"), sem("k_l")
        scr_w, qk_in = sem("scr_w"), sem("qk_in")
        ms_mm, mx_rd, mn_d, m_in = sem("ms_mm"), sem("mx_rd"), sem("mn_d"), sem("m_in")
        sc_mm, exp_d, pv_mm, nm_d = sem("sc_mm"), sem("exp_d"), sem("pv_mm"), sem("nm_d")
        rden_d, rdh_d, rdl_d, rb_mm, o_d = (sem(n) for n in ("rden_d", "rdh_d", "rdl_d", "rb_mm", "o_d"))
        xb_d, f_d = sem("xb_d"), sem("f_d")
        wo_mm, y_d, x2_d, x2c_d = sem("wo_mm"), sem("y_d"), sem("x2_d"), sem("x2c_d")
        g_mm, g_dl, g_ex, g_ch, sm_d = sem("g_mm"), sem("g_dl"), sem("g_ex"), sem("g_ch"), sem("sm_d")
        smt_mm, smt_cp, s_wr = sem("smt_mm"), sem("smt_cp"), sem("s_wr")
        s_in = [sem(f"s_in{k}") for k in range(NE // 2)]
        a_mm, b_mm, t_d, u_d, th_d, w_d, g_d = (sem(n) for n in ("a_mm", "b_mm", "t_d", "u_d", "th_d", "w_d", "g_d"))
        y_mm, fin_d, out_d = sem("y_mm"), sem("fin_d"), sem("out_d")

        NG = 11

        block = ctx.enter_context(nc.Block())

        def pipeline(eng, body):
            body(0, True, False)
            with eng.Fori(1, B - 1) as i:
                body(i, False, False)
            body(B - 1, False, True)

        def col(tile, k, b):
            return tile[:, k, bass.ds(b, 1)]

        @block.sync
        def _(sp):
            sp.dma_start(wqf, wqkv).then_inc(w_in, 16)
            sp.dma_start(ct[:], cT).then_inc(w_in, 16)
            sp.dma_start(wm, wmod).then_inc(w_in, 16)
            sp.dma_start(bia[:], bias).then_inc(w_in, 16)
            sp.dma_start(gw[:], gate).then_inc(w_in, 16)
            sp.dma_start(wof, wo).then_inc(w_in, 16)
            sp.dma_start(bob, borow.to_broadcast([B, D])).then_inc(w_in, 16)

            def load_x(b):
                if not (isinstance(b, int) and b == 0):
                    sp.wait_ge(xb_d, b)
                sp.dma_start(xt[:], x[bass.ds(b, 1)].rearrange("o (a p) d -> p (o a) d", p=128)).then_inc(x_in, 16)

            def regroup(b):
                sp.wait_ge(k_h, b + 1)
                sp.dma_start(k_scr[:, 0], kh[:].bitcast(F32)).then_inc(scr_w, 16)
                sp.dma_start(k_scr[:, 1], kh[:].bitcast(F32)).then_inc(scr_w, 16)
                sp.wait_ge(q_h, b + 1)
                sp.dma_start(q_scr[:, 0], qh[:].bitcast(F32)).then_inc(scr_w, 16)
                sp.dma_start(q_scr[:, 2], qh[:].bitcast(F32)).then_inc(scr_w, 16)
                sp.wait_ge(q_l, b + 1)
                sp.dma_start(q_scr[:, 1], ql[:].bitcast(F32)).then_inc(scr_w, 16)
                sp.wait_ge(k_l, b + 1)
                sp.dma_start(k_scr[:, 2], kl[:].bitcast(F32)).then_inc(scr_w, 16)
                sp.wait_ge(scr_w, 96 * b + 96)
                if isinstance(b, int) and b == 0:
                    sp.wait_ge(z_in, 2)
                    sp.wait_ge(scr0, 32)
                sp.dma_start(k4[:, :, WIN:WIN + S].bitcast(F32),
                             k_scr.rearrange("j c (d g) s -> (j c d) g s", g=HG)).then_inc(qk_in, 16)
                for j in range(HJ):
                    sp.dma_start(q4[32 * j:32 * j + 32, :, j, :].bitcast(F32),
                                 q_scr[j].rearrange("c (d g) s -> (c d) g s", g=HG)).then_inc(qk_in, 16)
                zeros = q_scr[0, 3, 0:4 * (HJ - 1), :].rearrange("(o g k) s -> o g (k s)", o=1, g=HG)
                sp.dma_start(q4[MROW:MROW + 1, :, 1:HJ, :].rearrange("o g j s -> o g (j s)").bitcast(F32),
                             zeros).then_inc(qk_in, 16)

            def put_max(b):
                sp.wait_ge(mn_d, b + 1)
                for gg in range(HG):
                    sp.dma_start(q4[MROW:MROW + 1, gg].rearrange("o j s -> o (j s)").bitcast(F32),
                                 mn[:, gg, :].bitcast(F32)).then_inc(m_in, 16)

            def spread_scores(b):
                sp.wait_ge(smt_cp, b + 1)
                sp.dma_start(s_scr, smT[:]).then_inc(s_wr, 16)
                sp.wait_ge(s_wr, 16 * b + 16)
                if isinstance(b, int) and b == 0:
                    sp.wait_ge(s_wl, 2)
                    sp.wait_ge(s_w2, 1)
                src = s_scr.rearrange("(o r) n -> o (r n)", o=1)
                for k in range(NE // 2):
                    if k == NE // 2 - 1 and not (isinstance(b, int) and b == 0):
                        sp.wait_ge(u_d, NX * b)
                    sp.dma_start(sbc[:, 2 * k:2 * k + 2, :].rearrange("p e s -> p (e s)"),
                                 src[:, 2 * k * S:2 * k * S + 2 * S].to_broadcast([128, 2 * S])).then_inc(s_in[k], 16)

            def store(b):
                sp.wait_ge(fin_d, b + 1)
                sp.dma_start(out[bass.ds(b, 1)].rearrange("o (a p) d -> p (o a) d", p=128), ot[:]).then_inc(out_d, 16)

            load_x(0)
            sp.wait_ge(cst_all, 1)
            sp.dma_start(k_scr[:, 3], g[:, 0]).then_inc(scr0, 16)
            sp.dma_start(q_scr[:, 3], g[:, 1]).then_inc(scr0, 16)
            sp.wait_ge(z_in, 1)
            for h in range(H):
                sp.dma_start(wom[DH * h:DH * h + DH, h % HJ, :], wo[DH * h:DH * h + DH, :]).then_inc(s_wom, 16)
            sp.dma_start(w13f, w13).then_inc(e_in, 16)
            sp.dma_start(w2f, w2).then_inc(e_in, 16)
            sp.wait_ge(s_mr, 1)
            sp.dma_start(m_scr, mrow[:]).then_inc(s_mw, 16)
            sp.wait_ge(s_mw, 16)
            src = m_scr.rearrange("(o b) k d -> o (b k d)", o=1).to_broadcast([128, B * 3 * D])
            sp.dma_start(mall[:].rearrange("p b k d -> p (b k d)"), src).then_inc(s_ma, 16)
            regroup(0)

            def body(b, first, last):
                if not last:
                    load_x(b + 1)
                put_max(b)
                if not last:
                    regroup(b + 1)
                spread_scores(b)
                if not first:
                    store(b - 1)

            pipeline(sp, body)
            store(B - 1)
            sp.wait_ge(out_d, 16 * B)

        @block.gpsimd
        def _(pool):
            made = [0]

            def const(ins):
                made[0] += 1
                ins.then_inc(cst, 1)
                pool.wait_ge(cst, made[0])

            def keep(tile, pattern, base, cm, op=ALU.is_ge, val=NEG):
                const(nc.gpsimd.affine_select(out=tile, in_=tile, compare_op=op, fill=val, base=base,
                                              pattern=pattern, channel_multiplier=cm))

            const(nc.gpsimd.memset(ident[:], 0.0))
            keep(ident[:], [[-1, 128]], 0, 1, ALU.not_equal, 1.0)
            const(nc.gpsimd.tensor_copy(identb[:], ident[:]))
            const(nc.gpsimd.memset(dsel[:], 0.0))
            for r in range(32 // NPB):
                keep(dsel[:, :, NPB * r:NPB * r + NPB], [[1, NPB], [-1, NPB]], 0, 0, ALU.not_equal, 1.0)
            const(nc.gpsimd.memset(rsel[:].bitcast(F32), 0.0))
            keep(rsel[:].rearrange("p k (c r) -> p k c r", c=HG), [[-1, NPB], [-32, HG], [0, 32]], 0, 1,
                 ALU.not_equal, 1.0)
            const(nc.gpsimd.memset(mhalf[:], -0.5))
            const(nc.gpsimd.memset(g[:, 0], 1.0))
            const(nc.gpsimd.memset(g[:, 1], 0.0))
            const(nc.gpsimd.iota(iota8[:], [[1, NE]], base=0, channel_multiplier=0,
                                 allow_small_or_imprecise_dtypes=True))
            const(nc.gpsimd.memset(mq[:], 0.0))
            const(nc.gpsimd.memset(mk[:], 0.0))
            for e in range(3):
                for j in range(HJ):
                    rows = mq[MB * j:MB * j + MB, e, :]
                    keep(rows, [[1, MK]], 0, -1)
                    keep(rows, [[-1, MK]], 2 * WIN, 1)
                keep(mk[:, e, :], [[-1, PB]], 0, 1)
                keep(mk[:, e, :], [[1, PB]], 2 * WIN, -1)
            keep(mq[:, 0, :], [[1, MK]], -WIN, 0)
            keep(mk[:, 0, :], [[0, PB]], -WIN, 1)
            keep(mq[:, 2, :], [[-1, MK]], MK - WIN - 1, 0)
            keep(mk[:, 2, :], [[0, PB]], 128 - WIN - 1, -1)
            nc.gpsimd.memset(zero[:], 0.0).then_inc(cst_all, 1)

            def inverse(b, s, ln):
                pool.wait_ge(s["ve"], b + 1)
                nc.gpsimd.tensor_tensor(ln["rstd"][:], ln["ve"][:], mhalf[:].to_broadcast([128, NQB]),
                                        ALU.pow).then_inc(s["rstd"], 1)

            def add_bias(b, first):
                if first:
                    pool.wait_ge(s_ma, 16)
                    pool.wait_ge(x_in, 16)
                else:
                    pool.wait_ge(x2_d, b)
                    pool.wait_ge(x_in, 16 * b + 16)
                nc.gpsimd.tensor_tensor(xb[:], xt[:], mall[:, bass.ds(b, 1), 2, :].to_broadcast([128, NQB, D]),
                                        ALU.add).then_inc(xb_d, 1)

            def low_h1(b):
                pool.wait_ge(l1["hh"], b + 1)
                nc.gpsimd.tensor_tensor(hlp[:, WIN:WIN + S], ln1["h"][:], hhp[:, WIN:WIN + S].bitcast(F32),
                                        ALU.subtract).then_inc(l1["hl"], 1)

            def low_qk(b):
                pool.wait_ge(q_h, b + 1)
                nc.gpsimd.tensor_tensor(ql[:], qf[:], qh[:].bitcast(F32), ALU.subtract).then_inc(q_l, 1)
                pool.wait_ge(k_h, b + 1)
                nc.gpsimd.tensor_tensor(kl[:], kf[:], kh[:].bitcast(F32), ALU.subtract).then_inc(k_l, 1)

            def keep_x2(b, first):
                pool.wait_ge(x2_d, b + 1)
                if not first:
                    pool.wait_ge(fin_d, b)
                nc.gpsimd.tensor_tensor(x2c[:].rearrange("p a d -> p (a d)"), x2[:].rearrange("p a d -> p (a d)"),
                                        zero[:].to_broadcast([128, S]), ALU.add).then_inc(x2c_d, 1)

            def expert(b, n, first):
                pool.wait_ge(u_d, NX * b + n + 1)
                nc.gpsimd.tensor_tensor(u[:, n % 2], t[:, n % 2], u[:, n % 2], ALU.mult).then_inc(w_d, 1)

            inverse(0, l1, ln1)
            low_h1(0)
            low_qk(0)
            add_bias(0, True)

            def body(b, first, last):
                if not first:
                    expert(b - 1, 3, False)
                    expert(b - 1, 4, False)
                if not last:
                    inverse(b + 1, l1, ln1)
                    low_h1(b + 1)
                if not first:
                    expert(b - 1, 5, False)
                inverse(b, l2, ln2)
                if not last:
                    low_qk(b + 1)
                for n in (6, 7, 8) if not first else ():
                    expert(b - 1, n, False)
                keep_x2(b, first)
                if not last:
                    add_bias(b + 1, False)
                for n in range(0, CSPLIT):
                    expert(b, n, first)

            pipeline(pool, body)
            for n in range(CSPLIT, NX):
                expert(B - 1, n, False)


        @block.scalar
        def _(act):
            act.wait_ge(w_in, 112)
            nc.scalar.activation(cth[:], ct[:], ACT.Tanh, scale=0.5).then_inc(s_th, 1)
            nc.scalar.activation(wqh[:], wqf, ACT.Copy).then_inc(s_wh, 1)
            act.wait_ge(e_in, 32)
            nc.scalar.activation(w13h[:], w13f, ACT.Copy).then_inc(s_wh, 1)
            nc.scalar.activation(w2s[:], w2f, ACT.Copy, scale=0.5).then_inc(s_w2, 1)

            def high_h1(b, first):
                act.wait_ge(l1["h"], b + 1)
                if not first:
                    act.wait_ge(v_mm, 2 * b)
                nc.scalar.activation(hhp[:, WIN:WIN + S], ln1["h"][:], ACT.Copy).then_inc(l1["hh"], 1)

            def high_qk(b, first):
                if not first:
                    act.wait_ge(scr_w, 96 * b)
                act.wait_ge(q_f, b + 1)
                nc.scalar.activation(qh[:], qf[:], ACT.Copy).then_inc(q_h, 1)
                act.wait_ge(k_f, b + 1)
                nc.scalar.activation(kh[:], kf[:], ACT.Copy).then_inc(k_h, 1)

            def copy_v(b, first):
                if not first:
                    act.wait_ge(pv_mm, NPB * b)
                for half, bank in ((0, "PV"), (1, "M0")):
                    act.wait_ge(v_mm, 2 * b + half + 1)
                    nc.scalar.activation(v[:, 4 * half:4 * half + 4, :], ps[bank][:], ACT.Copy).then_inc(v_ev, 1)

            def maxima(b, first):
                act.wait_ge(mx_rd, NMB * b + NMB)
                if not first:
                    act.wait_ge(m_in, 64 * b)
                nc.scalar.activation(mn[:], mx[:], ACT.Copy, scale=-1.0).then_inc(mn_d, 1)

            def sums(b, i):
                act.wait_ge(pv_mm, NPB * b + 2 * i + 2)
                if i == 0 and not (isinstance(b, int) and b == 0):
                    act.wait_ge(o_d, NPB // 2 * b)
                nc.scalar.activation(nm[:, 2 * i:2 * i + 2], ps["PV"][:], ACT.Copy).then_inc(nm_d, 1)

            def high_rden(b):
                act.wait_ge(rden_d, b + 1)
                nc.scalar.activation(rdh[:], rden[:], ACT.Copy).then_inc(rdh_d, 1)

            def probabilities(b):
                for n in range(NSC):
                    blk, half = n // 2, n % 2
                    act.wait_ge(sc_mm, NSC * b + n + 1)
                    if blk >= 2:
                        act.wait_ge(pv_mm, NPB * b + blk - 1)
                    nc.scalar.activation(p[:, blk % 2, 512 * half:512 * half + 512], sc_ps[n % 2][:],
                                         ACT.Exp).then_inc(exp_d, 1)
                    if n % 4 == 1 and n > 4:
                        sums(b, n // 4 - 1)
                sums(b, NPB // 2 - 1)

            def high_h2(b, first):
                act.wait_ge(l2["h"], b + 1)
                if not first:
                    act.wait_ge(b_mm, NX * b)
                nc.scalar.activation(h2h[:], ln2["h"][:], ACT.Copy).then_inc(l2["hh"], 1)

            def router_exp(b):
                act.wait_ge(g_dl, b + 1)
                nc.scalar.activation(ex[:], dl[:], ACT.Exp).then_inc(g_ex, 1)

            def router_scores(b, first):
                act.wait_ge(smt_mm, b + 1)
                if not first:
                    act.wait_ge(s_wr, 16 * b)
                nc.scalar.activation(smT[:], ps["M1"][0:NQB * NE, 0:QB], ACT.Copy).then_inc(smt_cp, 1)

            def expert(b, n, first):
                act.wait_ge(t_d, NX * b + n + 1)
                if n >= 2 or not first:
                    act.wait_ge(g_d, NX * b + max(n - 1, 0))
                nc.scalar.activation(th[:, n % 2], t[:, n % 2], ACT.Tanh, scale=0.5).then_inc(th_d, 1)

            high_h1(0, True)
            high_qk(0, True)
            copy_v(0, True)

            def body(b, first, last):
                maxima(b, first)
                if not first:
                    expert(b - 1, 3, False)
                    expert(b - 1, 4, False)
                probabilities(b)
                high_rden(b)
                if not last:
                    high_h1(b + 1, False)
                if not first:
                    expert(b - 1, 5, False)
                if not last:
                    high_qk(b + 1, False)
                    copy_v(b + 1, False)
                if not first:
                    expert(b - 1, 6, False)
                router_exp(b)
                if not first:
                    expert(b - 1, 7, False)
                    expert(b - 1, 8, False)
                router_scores(b, first)
                high_h2(b, first)
                for n in range(0, CSPLIT):
                    expert(b, n, first)

            pipeline(act, body)
            for n in range(CSPLIT, NX):
                expert(B - 1, n, False)

        @block.vector
        def _(dve):
            nc.vector.memset(wom[:], 0.0).then_inc(z_in, 1)
            nc.vector.memset(q4[:].bitcast(F32), 0.0)
            nc.vector.memset(k4[:].bitcast(F32), 0.0)
            nc.vector.memset(hhp[:].bitcast(F32), 0.0)
            nc.vector.memset(hlp[:].bitcast(F32), 0.0).then_inc(z_in, 1)
            dve.wait_ge(s_th, 1)
            nc.vector.scalar_tensor_tensor(cth[:], cth[:], 1.0, ct[:], ALU.add, ALU.mult).then_inc(s_sv, 1)
            dve.wait_ge(s_sv, 1)
            nc.vector.tensor_scalar(csl[:], cth[:], 0.5, None, ALU.mult).then_inc(s_sl, 1)
            dve.wait_ge(s_wh, 1)
            nc.vector.tensor_tensor(wql[:], wqf, wqh[:].bitcast(F32), ALU.subtract).then_inc(s_wl, 1)
            dve.wait_ge(s_mod, 1)
            pm = ps["M1"][:, 0:4 * B].rearrange("p (k b) -> p k b", k=4)
            nc.vector.tensor_copy(mod[:, 0:4:2], pm[:, 0:4:2])
            nc.vector.tensor_scalar(mod[:, 1:4:2], pm[:, 1:4:2], 1.0, None, ALU.add).then_inc(s_md, 1)
            dve.wait_ge(s_bo, 1)
            nc.vector.tensor_copy(mraw, ps["Y"][0:B, 0:2 * D]).then_inc(s_sv, 1)
            nc.vector.tensor_tensor(bo2, ps["Y"][0:B, 2 * D:3 * D], bob, ALU.add).then_inc(s_sv, 1)
            dve.wait_ge(s_sv, 3)
            nc.vector.tensor_scalar(mneg, mraw, -1.0, None, ALU.mult).then_inc(s_sv, 1)
            nc.vector.tensor_scalar(msgn, mraw, 0.0, 2.0, ALU.is_ge, ALU.mult).then_inc(s_sv, 1)
            dve.wait_ge(s_sv, 5)
            nc.vector.tensor_tensor(mabs, mneg, mraw, ALU.max).then_inc(s_sv, 1)
            dve.wait_ge(s_sv, 6)
            nc.vector.tensor_scalar(mneg, mabs, 0.25, None, ALU.max).then_inc(s_sv, 1)
            dve.wait_ge(s_sv, 7)
            nc.vector.scalar_tensor_tensor(mrow[:, 0:2], msgn, -1.0, mneg, ALU.add, ALU.mult).then_inc(s_sv, 1)
            dve.wait_ge(s_sv, 8)
            nc.vector.tensor_tensor(mrow[:, 2], mrow[:, 0], bo2, ALU.mult).then_inc(s_mr, 1)
            dve.wait_ge(s_md, 1)

            def statistics(b, s, ln, src):
                for a in range(NQB):
                    last = nc.vector.bn_stats(ln["st"][:, a], src[:, a])
                last.then_inc(s["bn"], 1)
                dve.wait_ge(s["bn"], 2 * b + 1)
                nc.vector.memset(spare[:], 0.0)
                for a in range(NQB):
                    last = nc.vector.bn_aggr(ln["mv"][:, a], ln["st"][:, a])
                last.then_inc(s["bn"], 1)
                dve.wait_ge(s["bn"], 2 * b + 2)
                nc.vector.tensor_scalar(ln["ve"][:], ln["mv"][:, :, 1], EPS, None, ALU.add).then_inc(s["ve"], 1)

            def normal(b, s, ln, src, first):
                dve.wait_ge(s["rstd"], b + 1)
                if not first:
                    dve.wait_ge(s["tr"], b)
                for a in range(NQB):
                    last = nc.vector.tensor_scalar(ln["xn"][:, a], src[:, a], ln["mv"][:, a, 0:1],
                                                   ln["rstd"][:, a:a + 1], ALU.subtract, ALU.mult)
                last.then_inc(s["xn"], 1)

            def modulate(b, s, ln, bank, k, first):
                dve.wait_ge(s["tr"], b + 1)
                if not first:
                    dve.wait_ge(s["hl"], b)
                nc.vector.tensor_scalar(ln["h"][:], ps[bank][:], col(mod, k + 1, b), col(mod, k, b),
                                        ALU.mult, ALU.add).then_inc(s["h"], 1)

            def bias_qk(b, first):
                dve.wait_ge(q_mm, b + 1)
                if not first:
                    dve.wait_ge(q_l, b)
                nc.vector.tensor_scalar(qf[:].rearrange("p (q n) -> p n q", n=NMB),
                                        ps["S0"][:].rearrange("p (n q) -> p n q", n=NMB), bia[:, 0:1], SCALE, ALU.add, ALU.mult).then_inc(q_f, 1)
                dve.wait_ge(k_mm, b + 1)
                if not first:
                    dve.wait_ge(k_l, b)
                nc.vector.tensor_scalar(kf[:], ps["S1"][:], bia[:, 1:2], None, ALU.add).then_inc(k_f, 1)

            def maxima(b, first):
                if not first:
                    dve.wait_ge(mn_d, b)
                for n in range(NMB):
                    dve.wait_ge(ms_mm, NMB * b + n + 1)
                    nc.vector.tensor_reduce(mx[:, :, n], mx_ps[n % 4][:, 0:HG * MK].rearrange("p (g k) -> p g k", g=HG),
                                            AX.X, ALU.max).then_inc(mx_rd, 1)

            def invert_sums(b):
                dve.wait_ge(pv_mm, NPB * b + NPB)
                nc.vector.reciprocal(rden[:], ps["M0"][:, 0:256]).then_inc(rden_d, 1)

            def low_rden(b):
                dve.wait_ge(rdh_d, b + 1)
                nc.vector.tensor_tensor(rdl[:], rden[:], rdh[:].bitcast(F32), ALU.subtract).then_inc(rdl_d, 1)

            def normalise(b, first):
                if not first:
                    dve.wait_ge(wo_mm, b)
                dve.wait_ge(nm_d, NPB // 2 * b + NPB // 2)
                for i in range(NPB // 2):
                    dve.wait_ge(rb_mm, NPB // 2 * b + i + 1)
                    nc.vector.tensor_tensor(
                        o[:, :, 2 * PB * i:2 * PB * i + 2 * PB].rearrange("p j (k q) -> p k j q", k=2),
                        nm[:, 2 * i:2 * i + 2], sc_ps[i % 2][:].rearrange("p (k j q) -> p k j q", k=2, j=HJ),
                        ALU.mult).then_inc(o_d, 1)

            def residual(b, first):
                dve.wait_ge(wo_mm, b + 1)
                if first:
                    dve.wait_ge(s_ma, 16)
                nc.vector.tensor_tensor(yt[:], ps["M1"][:].rearrange("p (a d) -> p a d", a=NQB),
                                        mall[:, bass.ds(b, 1), 0, :].to_broadcast([128, NQB, D]),
                                        ALU.mult).then_inc(y_d, 1)
                dve.wait_ge(y_d, b + 1)
                dve.wait_ge(xb_d, b + 1)
                if not first:
                    dve.wait_ge(x2c_d, b)
                nc.vector.tensor_tensor(x2[:], yt[:], xb[:], ALU.add).then_inc(x2_d, 1)
                dve.wait_ge(x2_d, b + 1)

            def router(b, part):
                done = [part]

                def link(ins):
                    done[0] += 1
                    ins.then_inc(g_ch, 1)
                    dve.wait_ge(g_ch, NG * b + done[0])

                lg = ps["M1"][:, 0:NQB * NE].rearrange("p (a e) -> p a e", a=NQB)
                bc = [128, NQB, NE]
                if part == 0:
                    dve.wait_ge(g_mm, b + 1)
                    link(nc.vector.tensor_reduce(rm[:], lg, AX.X, ALU.max))
                    nc.vector.tensor_tensor(dl[:], lg, rm[:].unsqueeze(2).to_broadcast(bc),
                                            ALU.subtract).then_inc(g_dl, 1)
                    return
                dve.wait_ge(g_ex, b + 1)
                link(nc.vector.tensor_reduce(es[:], ex[:], AX.X, ALU.add))
                link(nc.vector.reciprocal(er[:], es[:]))
                link(nc.vector.tensor_tensor(sc[:], ex[:], er[:].unsqueeze(2).to_broadcast(bc), ALU.mult))
                nc.vector.memset(spare[:], 0.0)
                for a in range(NQB):
                    last = nc.vector.max(m8[:, a, :], sc[:, a, :])
                link(last)
                nc.vector.memset(spare[:], 0.0)
                for a in range(NQB):
                    last = nc.vector.max_index(ix[:, a, :], m8[:, a, :], sc[:, a, :])
                link(last)
                link(nc.vector.tensor_copy(ixf[:], ix[:, :, 0:2]))
                for r in range(2):
                    link(nc.vector.tensor_tensor(sel[:, r], iota8[:].unsqueeze(1).to_broadcast(bc),
                                                 ixf[:, :, r:r + 1].to_broadcast(bc), ALU.is_equal))
                link(nc.vector.tensor_tensor(selb[:], sel[:, 0], sel[:, 1], ALU.add))
                nc.vector.tensor_tensor(sm[:].rearrange("p e a -> p a e"), sc[:], selb[:], ALU.mult).then_inc(g_ch, 1)
                assert done[0] + 1 == NG

            def gate_w(b, n, dst, bank, buf):
                if n == 0:
                    return nc.vector.tensor_copy(dst[:, buf], ps[bank][:])
                return nc.vector.tensor_tensor(dst[:, buf], ps[bank][:], sbc[:, n - 1], ALU.mult)

            def combine(b, n, first):
                dve.wait_ge(th_d, NX * b + n + 1)
                dve.wait_ge(w_d, NX * b + n + 1)
                if n >= 2 or not first:
                    dve.wait_ge(y_mm, NX * b + max(n - 1, 0))
                nc.vector.scalar_tensor_tensor(g[:, n % 2], th[:, n % 2], 1.0, u[:, n % 2],
                                               ALU.add, ALU.mult).then_inc(g_d, 1)

            def expert(b, n, first):
                dve.wait_ge(a_mm, NX * b + n + 1)
                if n % 2 == 1:
                    dve.wait_ge(s_in[n // 2], 16 * b + 16)
                if n >= 2 or not first:
                    dve.wait_ge(w_d, NX * b + max(n - 1, 0))
                    dve.wait_ge(th_d, NX * b + max(n - 1, 0))
                gate_w(b, n, t, "A", n % 2).then_inc(t_d, 1)
                if n >= 2 or not first:
                    dve.wait_ge(g_d, NX * b + max(n - 1, 0))
                dve.wait_ge(b_mm, NX * b + n + 1)
                gate_w(b, n, u, "B", n % 2).then_inc(u_d, 1)
                if n >= 1:
                    combine(b, n - 1, first)

            def finish(b, first):
                combine(b, NX - 1, False)
                dve.wait_ge(y_mm, NX * b + NX)
                nc.vector.tensor_tensor(yt[:], ps["Y"][:].rearrange("p (a d) -> p a d", a=NQB),
                                        mall[:, bass.ds(b, 1), 1, :].to_broadcast([128, NQB, D]),
                                        ALU.mult).then_inc(f_d, 1)
                dve.wait_ge(f_d, b + 1)
                dve.wait_ge(x2c_d, b + 1)
                if not first:
                    dve.wait_ge(out_d, 16 * b)
                nc.vector.tensor_tensor(ot[:], yt[:], x2c[:], ALU.add).then_inc(fin_d, 1)

            def low_h2(b):
                dve.wait_ge(l2["hh"], b + 1)
                nc.vector.tensor_tensor(h2l[:], ln2["h"][:], h2h[:].bitcast(F32), ALU.subtract).then_inc(l2["hl"], 1)

            def split_experts():
                dve.wait_ge(s_wh, 2)
                nc.vector.tensor_tensor(w13l[:], w13f, w13h[:].bitcast(F32), ALU.subtract).then_inc(s_wl, 1)

            dve.wait_ge(x_in, 16)
            statistics(0, l1, ln1, xt)
            normal(0, l1, ln1, xt, True)
            modulate(0, l1, ln1, "M1", 0, True)
            bias_qk(0, True)
            split_experts()

            def body(b, first, last):
                maxima(b, first)
                if not first:
                    expert(b - 1, 3, False)
                    expert(b - 1, 4, False)
                if not last:
                    dve.wait_ge(x_in, 16 * b + 32)
                    statistics(b + 1, l1, ln1, xt)
                    normal(b + 1, l1, ln1, xt, False)
                invert_sums(b)
                if not last:
                    modulate(b + 1, l1, ln1, "M1", 0, False)
                low_rden(b)
                if not first:
                    expert(b - 1, 5, False)
                normalise(b, first)
                residual(b, first)
                statistics(b, l2, ln2, x2)
                if not last:
                    bias_qk(b + 1, False)
                normal(b, l2, ln2, x2, first)
                modulate(b, l2, ln2, "M1", 2, first)
                if not first:
                    expert(b - 1, 6, False)
                router(b, 0)
                if not first:
                    expert(b - 1, 7, False)
                router(b, 1)
                if not first:
                    expert(b - 1, 8, False)
                low_h2(b)
                if not first:
                    finish(b - 1, False)
                for n in range(0, CSPLIT):
                    expert(b, n, first)

            pipeline(dve, body)
            for n in range(CSPLIT, NX):
                expert(B - 1, n, False)
            finish(B - 1, False)

        @block.tensor
        def _(pe):
            mm = nc.tensor.matmul

            heads = q4[:].rearrange("p g j s -> p g (j s)")
            queries = q4[:].rearrange("p g j (q n) -> p g j q n", n=NMB)

            def exact3(dst, wh, wl, xh, xl):
                mm(dst, wh, xh, start=True, stop=False)
                mm(dst, wl, xh, start=False, stop=False)
                return mm(dst, wh, xl, start=False, stop=True)

            pe.wait_ge(w_in, 112)
            pe.wait_ge(cst_all, 1)
            pe.wait_ge(s_sl, 1)
            for i, k in enumerate((0, 1, 3, 4)):
                last = mm(ps["M1"][:, i * B:i * B + B], wm[:, k, :], csl[:], start=True, stop=True)
            last.then_inc(s_mod, 1)
            for i, k in enumerate((2, 5)):
                mm(ps["Y"][0:B, i * D:i * D + D], csl[:], wm[:, k, :], start=True, stop=True)
            mm(ps["Y"][0:B, 2 * D:3 * D], bia[:, 2:3].to_broadcast([128, B]), wof, start=True, stop=True)\
                .then_inc(s_bo, 1)

            def flip(b, s, ln, bank):
                pe.wait_ge(s["xn"], b + 1)
                for a in range(NQB):
                    last = nc.tensor.transpose(ps[bank][:, QB * a:QB * a + QB], ln["xn"][:, a], ident[:])
                last.then_inc(s["tr"], 1)

            def project(b, first):
                pe.wait_ge(l1["hl"], b + 1)
                if not first:
                    pe.wait_ge(exp_d, NSC * b)
                    pe.wait_ge(o_d, NPB // 2 * b)
                hh, hl = hhp[:, WIN:WIN + S], hlp[:, WIN:WIN + S]
                exact3(ps["S0"][:], wqh[:, 0, :], wql[:, 0, :], hh, hl).then_inc(q_mm, 1)
                exact3(ps["S1"][:], wqh[:, 1, :], wql[:, 1, :], hh, hl).then_inc(k_mm, 1)
                for half, bank in ((0, "PV"), (1, "M0")):
                    for i in range(4):
                        win = slice(PB * (4 * half + i), PB * (4 * half + i) + 128)
                        dst = ps[bank][:, 128 * i:128 * i + 128]
                        mm(dst, hhp[:, win], wqh[:, 2, :], start=True, stop=False)
                        mm(dst, hhp[:, win], wql[:, 2, :], start=False, stop=False)
                        last = mm(dst, hlp[:, win], wqh[:, 2, :], start=False, stop=True)
                    last.then_inc(v_mm, 1)

            def maxima(b, first):
                pe.wait_ge(qk_in, 96 * b + 96)
                for n in range(NMB):
                    edge = 0 if n == 0 else 2 if n == NMB - 1 else 1
                    if n == 2:
                        pe.wait_ge(v_ev, 2 * b + 2)
                    if n >= 4:
                        pe.wait_ge(mx_rd, NMB * b + n - 3)
                    bank = mx_ps[n % 4]
                    mm(bank[:, 0:HG * MK], identb[:], mq[:, edge, :].unsqueeze(1).to_broadcast([128, HG, MK]),
                       start=True, stop=False)
                    for gg in range(HG):
                        last = mm(bank[:, MK * gg:MK * gg + MK], heads[:, gg, n:NMB * (HJ * MB - 1) + n + 1:NMB],
                                  k4[:, gg, MB * n:MB * n + MK], start=False, stop=gg == HG - 1)
                    last.then_inc(ms_mm, 1)

            def values(b, blk):
                pe.wait_ge(exp_d, NSC * b + 2 * blk + 2)
                if blk == 0:
                    pe.wait_ge(v_ev, 2 * b + 2)
                elif blk % 2 == 0:
                    pe.wait_ge(nm_d, NPB // 2 * b + blk // 2)
                for c in range(HG):
                    r = slice(32 * c, 32 * c + 32)
                    mm(ps["PV"][r, 256 * (blk % 2):256 * (blk % 2) + 256], v[:, blk, r],
                       p[:, blk % 2, 256 * c:256 * c + 256], start=True, stop=True)
                for c in range(HG):
                    r = slice(32 * c, 32 * c + 32)
                    last = mm(ps["M0"][r, 0:256], dsel[:, blk, :], p[:, blk % 2, 256 * c:256 * c + 256],
                              start=blk == 0, stop=blk == NPB - 1)
                last.then_inc(pv_mm, 1)

            def scores(b):
                pe.wait_ge(m_in, 64 * b + 64)
                for blk in range(NPB):
                    edge = 0 if blk == 0 else 2 if blk == NPB - 1 else 1
                    for half in range(2):
                        n = 2 * blk + half
                        if n >= 2:
                            pe.wait_ge(exp_d, NSC * b + n - 1)
                        bank = sc_ps[n % 2]
                        mm(bank[:], identb[:], mk[:, edge, :].unsqueeze(1).to_broadcast([128, 8, PB]),
                           start=True, stop=False)
                        for a in range(2):
                            gg = 2 * half + a
                            last = mm(bank[:, 256 * a:256 * a + 256], k4[:, gg, PB * blk:PB * blk + 128],
                                      queries[:, gg, :, :, 2 * blk:2 * blk + 2].rearrange("p j q n -> p j n q"), start=False, stop=a == 1)
                        last.then_inc(sc_mm, 1)
                    if blk >= 1:
                        values(b, blk - 1)
                values(b, NPB - 1)

            def spread_rden(b):
                pe.wait_ge(rdl_d, b + 1)
                for i in range(NPB // 2):
                    if i >= 2:
                        pe.wait_ge(o_d, NPB // 2 * b + i - 1)
                    for k in range(2):
                        dst = sc_ps[i % 2][:, 256 * k:256 * k + 256]
                        mm(dst, rsel[:, 2 * i + k, :], rdh[:], start=True, stop=False)
                        last = mm(dst, rsel[:, 2 * i + k, :], rdl[:], start=False, stop=True)
                    last.then_inc(rb_mm, 1)

            def attn_out(b):
                pe.wait_ge(o_d, NPB // 2 * b + NPB // 2)
                for a in range(NQB):
                    for j in range(HJ):
                        last = mm(ps["M1"][:, QB * a:QB * a + QB], o[:, j, QB * a:QB * a + QB], wom[:, j, :],
                                  start=j == 0, stop=j == HJ - 1)
                last.then_inc(wo_mm, 1)

            def router(b):
                pe.wait_ge(l2["h"], b + 1)
                for a in range(NQB):
                    last = mm(ps["M1"][:, NE * a:NE * a + NE], ln2["h"][:, QB * a:QB * a + QB], gw[:],
                              start=True, stop=True)
                last.then_inc(g_mm, 1)

            def router_t(b):
                pe.wait_ge(g_ch, NG * b + NG)
                nc.tensor.transpose(ps["M1"][0:NQB * NE, 0:QB], sm[:].rearrange("p e a -> p (e a)"),
                                    ident[:]).then_inc(smt_mm, 1)

            def down(b, n, first):
                pe.wait_ge(g_d, NX * b + n + 1)
                if n == 0 and not first:
                    pe.wait_ge(fin_d, b)
                e = (n - 1) % NX
                for a in range(NQB):
                    last = mm(ps["Y"][:, QB * a:QB * a + QB], g[:, n % 2, QB * a:QB * a + QB], w2s[:, e, :],
                              start=n == 0 and a == 0, stop=n == NX - 1, skip_group_check=True)
                last.then_inc(y_mm, 1)

            def expert(b, n, first):
                e = (n - 1) % NX
                if n == 0:
                    pe.wait_ge(l2["hl"], b + 1)
                if n >= 1 or not first:
                    pe.wait_ge(t_d, NX * b + n)
                exact3(ps["A"][:], w13h[:, e, 0, :], w13l[:, e, 0, :], h2h[:], h2l[:]).then_inc(a_mm, 1)
                if n >= 1 or not first:
                    pe.wait_ge(u_d, NX * b + n)
                exact3(ps["B"][:], w13h[:, e, 1, :], w13l[:, e, 1, :], h2h[:], h2l[:]).then_inc(b_mm, 1)
                if n >= 2:
                    down(b, n - 2, first)

            pe.wait_ge(s_md, 1)
            flip(0, l1, ln1, "M1")
            pe.wait_ge(s_wl, 1)
            pe.wait_ge(z_in, 2)
            project(0, True)
            pe.wait_ge(s_wom, 16 * H)

            def body(b, first, last):
                maxima(b, first)
                if not first:
                    expert(b - 1, 3, False)
                    expert(b - 1, 4, False)
                scores(b)
                if not last:
                    if not first:
                        pe.wait_ge(smt_cp, b)
                    flip(b + 1, l1, ln1, "M1")
                if not first:
                    expert(b - 1, 5, False)
                spread_rden(b)
                if not last:
                    pe.wait_ge(l1["h"], b + 2)
                attn_out(b)
                if not last:
                    project(b + 1, False)
                flip(b, l2, ln2, "M1")
                if not first:
                    expert(b - 1, 6, False)
                router(b)
                if not first:
                    expert(b - 1, 7, False)
                    expert(b - 1, 8, False)
                router_t(b)
                if not first:
                    down(b - 1, NX - 2, False)
                    down(b - 1, NX - 1, False)
                else:
                    pe.wait_ge(s_wl, 2)
                    pe.wait_ge(s_w2, 1)
                for n in range(0, CSPLIT):
                    expert(b, n, first)

            pipeline(pe, body)
            for n in range(CSPLIT, NX):
                expert(B - 1, n, False)
            down(B - 1, NX - 2, False)
            down(B - 1, NX - 1, False)


CSPLIT = 3


def kernel(**inputs):
    import concourse.bacc as bacc
    from concourse.bass_utils import run_bass_kernel_spmd

    a = {k: np.asarray(x) for k, x in inputs.items()}
    order = np.arange(D).reshape(HG, HJ, DH).transpose(1, 2, 0).reshape(-1)
    lay = {
        "x": a["L0_attn_x"],
        "w13": np.stack([np.concatenate([a["L0_ffn_w1"], a["L0_ffn_w1s"]]),
                         np.concatenate([a["L0_ffn_w3"], a["L0_ffn_w3s"]])]).transpose(2, 1, 0, 3),
        "w2": np.concatenate([a["L0_ffn_w2"], a["L0_ffn_w2s"]]).transpose(1, 0, 2),
        "wqkv": np.stack([a["L0_attn_wq"][order], a["L0_attn_wk"][order], a["L0_attn_wv"]]).transpose(2, 0, 1),
        "wo": a["L0_attn_wo"].T,
        "gate": a["L0_ffn_gate_w"].T,
        "bias": np.stack([a["L0_attn_bq"][order], a["L0_attn_bk"][order], a["L0_attn_bv"], a["L0_attn_bo"]]).T,
        "borow": a["L0_attn_bo"][None],
        "cT": a["L0_c"].T,
        "wmod": a["L0_wmod"].reshape(D, 6, D),
    }
    nc = bacc.Bacc("TRN2", target_bir_lowering=False, num_devices=1)
    arrays, args = {}, []
    for name, x in lay.items():
        arrays[name] = np.ascontiguousarray(x)
        args.append(nc.dram_tensor(name, x.shape, F32, kind="ExternalInput").ap())
    args.append(nc.dram_tensor("out", (B, S, D), F32, kind="ExternalOutput").ap())
    build(nc, *args)
    r = run_bass_kernel_spmd(nc, [arrays], core_ids=[0])
    return r.results[0]["out"]
```

```python
import numpy as np
import concourse.bass as bass
from concourse import mybir
from contextlib import ExitStack

F32 = mybir.dt.float32
F32R = mybir.dt.float32r
BF16 = mybir.dt.bfloat16
U32 = mybir.dt.uint32
ALU = mybir.AluOpType
ACT = mybir.ActivationFunctionType
AX = mybir.AxisListType

B, S, D = 16, 512, 128
H, DH = 16, 8
HG, HJ = 4, 4
WIN = 32
NE = 8
SCALE = DH ** -0.5
EPS = 1e-5
NEG = -1e30

QB = 128
NQB = S // QB
MB = 32
MK = MB + 2 * WIN
NMB = S // MB
PB = 64
NPB = S // PB
SPAD = S + 2 * WIN
NSC = NPB * 2
NX = NE + 1
MROW = 3 * DH

FILL = {
    "maxima": (0, 1, 2, 3),
    "sums": (4,),
    "division": (5,),
    "norm": (6,),
    "features": (7,),
    "router": (8,),
}
NP = 3
PE_MASKS = (1, 3, 5)
CSPLIT = 2


def ln_sems(sem, name):
    return {k: sem(f"{name}_{k}") for k in ("bn", "ve", "rstd", "xn", "tr", "h", "hh", "hl")}


def build(nc, x, w13, w2, wqkv, wo, gate, bias, borow, cT, wmod, out):
    ctx = ExitStack()
    with ctx:
        def sb(name, shape, dt=F32):
            return ctx.enter_context(nc.sbuf_tensor(name, shape, dt))

        def sem(name):
            return ctx.enter_context(nc.semaphore(name))

        q_scr = nc.dram_tensor("q_scr", (HJ, 3, 32, S), F32, kind="Internal").ap()
        zeros = nc.dram_tensor("zeros", (HG, HJ * S), F32, kind="Internal").ap()
        k_scr = nc.dram_tensor("k_scr", (HJ, 4, 32, S), F32, kind="Internal").ap()
        m_scr = nc.dram_tensor("m_scr", (B, 3, D), F32, kind="Internal").ap()
        s_scr = nc.dram_tensor("s_scr", (NQB * NE, QB), F32, kind="Internal").ap()

        w13h = sb("w13h", [128, NX, 2, 128], F32R)
        w13l = sb("w13l", [128, NX, 2, 128], F32R)
        w2s = sb("w2s", [128, NX, 128])
        wqh = sb("wqh", [128, 3, 128], F32R)
        wql = sb("wql", [128, 3, 128], F32R)
        wom = sb("wom", [128, HJ, 128])
        womg = sb("womg", [128, HJ, 128])
        gw = sb("gw", [128, NE])
        bia = sb("bia", [128, 4])
        ct = sb("ct", [128, B])
        cth = sb("cth", [128, B])
        csl = sb("csl", [128, B])
        mod = sb("mod", [128, 4, B])
        mrow = sb("mrow", [B, 3, D])
        mall = sb("mall", [128, B, 3, D])
        ident = sb("ident", [128, 128])
        identb = sb("identb", [128, 128], BF16)
        dsel = sb("dsel", [128, NPB, 32])
        lowrow = sb("lowrow", [128, 1])
        rsel = sb("rsel", [128, NPB, 128], F32R)
        mhalf = sb("mhalf", [128, 1])
        zero = sb("zero", [128, 1])
        spare = sb("spare", [128, 1])
        iota8 = sb("iota8", [128, NE])
        mq = sb("mq", [128, 3, MK], BF16)
        mk = sb("mk", [128, 3, PB], BF16)
        cap = sb("cap", [128, 3, PB])
        xt = sb("xt", [128, NQB, D])
        xb = sb("xb", [128, NQB, D])
        xn = sb("xn", [128, NQB, D])

        def ln_tiles(name):
            return {"st": sb(name + "_st", [128, NQB, 6]), "mv": sb(name + "_mv", [128, NQB, 2]),
                    "ve": sb(name + "_ve", [128, NQB]), "rstd": sb(name + "_rstd", [128, NQB]),
                    "xn": xn, "h": sb(name + "_h", [128, S])}

        ln1, ln2 = ln_tiles("l1"), ln_tiles("l2")
        hhp = sb("hhp", [128, SPAD], F32R)
        hlp = sb("hlp", [128, SPAD], F32R)
        bqs = sb("bqs", [128, 1])
        qh, ql = sb("qh", [128, S], F32R), sb("ql", [128, S], F32R)
        kh, kl = sb("kh", [128, S], F32R), sb("kl", [128, S], F32R)
        vf = sb("vf", [128, SPAD])
        v = sb("v", [128, NPB, 128])
        q4 = sb("q4", [128, HG, HJ, S], F32R)
        k4 = sb("k4", [128, HG, SPAD], F32R)
        mx = sb("mx", [128, HG, NMB])
        mn = sb("mn", [128, HG, NMB], F32R)
        p = sb("p", [128, NP, H * PB])
        rdh, rdx = sb("rdh", [128, HJ * PB], F32R), sb("rdx", [128, HJ * PB], F32R)
        rden = sb("rden", [128, HJ * PB])
        o = sb("o", [128, HJ, S])
        yt = sb("yt", [128, NQB, D])
        x2 = sb("x2", [128, NQB, D])
        h2h = sb("h2h", [128, S], F32R)
        h2l = sb("h2l", [128, S], F32R)
        rm, dl, ex = sb("rm", [128, NQB]), sb("dl", [128, NQB, NE]), sb("ex", [128, NQB, NE])
        es, er, sc = sb("es", [128, NQB]), sb("er", [128, NQB]), sb("sc", [128, NQB, NE])
        m8 = sb("m8", [128, NQB, 8])
        ix = sb("ix", [128, NQB, 8], U32)
        ixf = sb("ixf", [128, NQB, 2])
        sel = sb("sel", [128, 2, NQB, NE])
        selb = sb("selb", [128, NQB, NE])
        sm = sb("sm", [128, NE, NQB])
        smT = sb("smT", [NQB * NE, QB])
        sbc = sb("sbc", [128, NE, S])
        start_o = o[:].rearrange("p j s -> p (j s)")
        wm = start_o[:, 0:6 * D].rearrange("p (k d) -> p k d", k=6)
        wqf = start_o[:, 6 * D:9 * D].rearrange("p (k d) -> p k d", k=3)
        wof = start_o[:, 9 * D:10 * D]
        start_n = p[0:B].rearrange("p k n -> p (k n)")
        mraw, mneg, mabs, msgn = (start_n[:, 2 * D * i:2 * D * i + 2 * D].rearrange("p (k d) -> p k d", k=2)
                                  for i in range(4))
        bob, bo2 = start_n[:, 8 * D:9 * D], start_n[:, 9 * D:10 * D]
        land = sbc[:].rearrange("p e s -> p (e s)")
        w13f = land[:, 0:NX * 256].rearrange("p (e k n) -> p e k n", e=NX, k=2)
        w2f = land[:, NX * 256:NX * 384].rearrange("p (e n) -> p e n", e=NX)
        x2c = sb("x2c", [128, NQB, D])
        t, u = sb("t", [128, 2, S]), sb("u", [128, 2, S])
        th = sb("th", [128, 2, S])
        g = sb("g", [128, 2, S])

        ps = {n: ctx.enter_context(nc.psum_tensor(f"ps_{n}", [128, 512], F32))
              for n in ("S0", "S1", "PV", "A", "B", "Y", "M0", "M1")}
        sc_ps = (ps["S0"], ps["S1"])
        pv_ps = (ps["M1"], ps["PV"])
        rb_ps = (ps["S0"], ps["S1"], ps["PV"], ps["M0"])
        mx_ps = (ps["PV"], ps["M0"], ps["S0"], ps["S1"])

        ab_ps = {n: (ps["A"], ps["B"]) for n in range(NX)}
        ab_ps[2] = (ps["PV"], ps["M0"])
        ab_ps[7] = (ps["S0"], ps["S1"])

        w_in = sem("w_in")
        e_in = sem("e_in")
        cst = sem("cst")
        cst_all = sem("cst_all")
        z_in = sem("z_in")
        scr0 = sem("scr0")
        s_th = sem("s_th")
        s_sv = sem("s_sv")
        s_sl = sem("s_sl")
        s_mod = sem("s_mod")
        s_md = sem("s_md")
        s_bo = sem("s_bo")
        s_mr = sem("s_mr")
        s_mw = sem("s_mw")
        s_ma = sem("s_ma")
        s_wom = sem("s_wom")
        s_wh = sem("s_wh")
        s_wl = sem("s_wl")
        s_w2 = sem("s_w2")
        s_bq = sem("s_bq")
        l1, l2 = ln_sems(sem, "l1"), ln_sems(sem, "l2")
        x_in = sem("x_in")
        xb_d = sem("xb_d")
        q_mm, k_mm = sem("q_mm"), sem("k_mm")
        q_h, k_h = sem("q_h"), sem("k_h")
        q_l, k_l = sem("q_l"), sem("k_l")
        vf_mm, vf_d = sem("vf_mm"), sem("vf_d")
        v_mm, v_ev = sem("v_mm"), sem("v_ev")
        q_scr_w, k_scr_w = sem("q_scr_w"), sem("k_scr_w")
        qk_in = sem("qk_in")
        ms_mm = sem("ms_mm")
        mx_rd = sem("mx_rd")
        mn_d = sem("mn_d")
        m_in = sem("m_in")
        sc_mm = sem("sc_mm")
        exp_d = sem("exp_d")
        p_d = sem("p_d")
        pv_mm = sem("pv_mm")
        nm_d = sem("nm_d")
        rden_d = sem("rden_d")
        rdh_d, rdx_d = sem("rdh_d"), sem("rdx_d")
        rb_mm = sem("rb_mm")
        o_d = sem("o_d")
        wg_d = sem("wg_d")
        wo_mm = sem("wo_mm")
        x2_d = sem("x2_d")
        x2c_d = sem("x2c_d")
        g_mm = sem("g_mm")
        g_dl, g_ex = sem("g_dl"), sem("g_ex")
        g_ch = sem("g_ch")
        smt_mm, smt_cp = sem("smt_mm"), sem("smt_cp")
        s_wr = sem("s_wr")
        s_in = [sem(f"s_in{k}") for k in range(NE // 2)]
        a_mm, b_mm = sem("a_mm"), sem("b_mm")
        t_d, u_d = sem("t_d"), sem("u_d")
        th_d = sem("th_d")
        w_d = sem("w_d")
        g_d = sem("g_d")
        y_mm = sem("y_mm")
        f_d = sem("f_d")
        fin_d = sem("fin_d")
        out_d = sem("out_d")

        IDENT, PLANES = 3, 5
        MASKS = PLANES + 3 + 2 * HJ
        NG = 11

        block = ctx.enter_context(nc.Block())

        def fill(expert, b, place, first):
            if not first:
                for n in FILL[place]:
                    if n >= CSPLIT:
                        expert(b - 1, n, False)

        def pair_of_blocks(i):
            return o[:, :, 2 * PB * i:2 * PB * i + 2 * PB].rearrange("p j (k q) -> p k j q", k=2)

        def pipeline(eng, body):
            body(0, True, False)
            with eng.Fori(1, B - 1) as i:
                body(i, False, False)
            body(B - 1, False, True)

        def col(tile, k, b):
            return tile[:, k, bass.ds(b, 1)]

        @block.sync
        def _(sp):
            sp.dma_start(wqf, wqkv).then_inc(w_in, 16)
            sp.dma_start(ct[:], cT).then_inc(w_in, 16)
            sp.dma_start(wm, wmod).then_inc(w_in, 16)
            sp.dma_start(bia[:], bias).then_inc(w_in, 16)
            sp.dma_start(gw[:], gate).then_inc(w_in, 16)
            sp.dma_start(wof, wo).then_inc(w_in, 16)
            sp.dma_start(bob, borow.to_broadcast([B, D])).then_inc(w_in, 16)

            def load_x(b):
                if not (isinstance(b, int) and b == 0):
                    sp.wait_ge(xb_d, b)
                sp.dma_start(xt[:], x[bass.ds(b, 1)].rearrange("o (a p) d -> p (o a) d", p=128)).then_inc(x_in, 16)

            def regroup(b):
                sp.wait_ge(q_h, b + 1)
                sp.dma_start(q_scr[:, 0], qh[:].bitcast(F32)).then_inc(q_scr_w, 16)
                sp.dma_start(q_scr[:, 2], qh[:].bitcast(F32)).then_inc(q_scr_w, 16)
                sp.wait_ge(q_l, b + 1)
                sp.dma_start(q_scr[:, 1], ql[:].bitcast(F32)).then_inc(q_scr_w, 16)
                sp.wait_ge(k_h, b + 1)
                sp.dma_start(k_scr[:, 0], kh[:].bitcast(F32)).then_inc(k_scr_w, 16)
                sp.dma_start(k_scr[:, 1], kh[:].bitcast(F32)).then_inc(k_scr_w, 16)
                sp.wait_ge(k_l, b + 1)
                sp.dma_start(k_scr[:, 2], kl[:].bitcast(F32)).then_inc(k_scr_w, 16)
                if isinstance(b, int) and b == 0:
                    sp.wait_ge(z_in, 3)
                    sp.wait_ge(scr0, 32)
                sp.dma_start(q4[MROW:MROW + 1].rearrange("o g j s -> o g (j s)").bitcast(F32),
                             zeros.rearrange("(o g) n -> o g n", o=1)).then_inc(qk_in, 16)
                sp.wait_ge(q_scr_w, 48 * b + 48)
                for j in range(HJ):
                    sp.dma_start(q4[32 * j:32 * j + 3 * DH, :, j, :].bitcast(F32),
                                 q_scr[j].rearrange("c (d g) s -> (c d) g s", g=HG)).then_inc(qk_in, 16)
                sp.wait_ge(k_scr_w, 48 * b + 48)
                sp.dma_start(k4[:, :, WIN:WIN + S].bitcast(F32),
                             k_scr.rearrange("j c (d g) s -> (j c d) g s", g=HG)).then_inc(qk_in, 16)

            def put_max(b):
                sp.wait_ge(mn_d, b + 1)
                for gg in range(HG):
                    sp.dma_start(q4[MROW:MROW + 1, gg].rearrange("o j s -> o (j s)").bitcast(F32),
                                 mn[:, gg, :].bitcast(F32)).then_inc(m_in, 16)

            def spread_scores(b):
                sp.wait_ge(smt_cp, b + 1)
                sp.dma_start(s_scr, smT[:]).then_inc(s_wr, 16)
                sp.wait_ge(s_wr, 16 * b + 16)
                if isinstance(b, int) and b == 0:
                    sp.wait_ge(s_wl, 2)
                    sp.wait_ge(s_w2, 1)
                src = s_scr.rearrange("(o r) n -> o (r n)", o=1)
                for k in range(NE // 2):
                    if k == NE // 2 - 1 and not (isinstance(b, int) and b == 0):
                        sp.wait_ge(u_d, NX * b)
                    sp.dma_start(sbc[:, 2 * k:2 * k + 2, :].rearrange("p e s -> p (e s)"),
                                 src[:, 2 * k * S:2 * k * S + 2 * S].to_broadcast([128, 2 * S])).then_inc(s_in[k], 16)

            def store(b):
                sp.wait_ge(fin_d, b + 1)
                sp.dma_start(out[bass.ds(b, 1)].rearrange("o (a p) d -> p (o a) d", p=128), yt[:]).then_inc(out_d, 16)

            load_x(0)
            sp.dma_start(w13f, w13).then_inc(e_in, 16)
            sp.dma_start(w2f, w2).then_inc(e_in, 16)
            sp.wait_ge(cst, PLANES)
            sp.dma_start(k_scr[:, 3], g[:, 0]).then_inc(scr0, 16)
            sp.dma_start(zeros.rearrange("g (a n) -> (g a) n", n=S), g[0:HG * HJ, 1]).then_inc(scr0, 16)
            regroup(0)
            sp.wait_ge(s_mr, 1)
            sp.dma_start(m_scr, mrow[:]).then_inc(s_mw, 16)
            sp.wait_ge(s_mw, 16)
            src = m_scr.rearrange("(o b) k d -> o (b k d)", o=1).to_broadcast([128, B * 3 * D])
            sp.dma_start(mall[:].rearrange("p b k d -> p (b k d)"), src).then_inc(s_ma, 16)
            sp.wait_ge(z_in, 1)
            for h in range(H):
                sp.dma_start(wom[DH * h:DH * h + DH, h % HJ, :], wo[DH * h:DH * h + DH, :]).then_inc(s_wom, 16)
            put_max(0)

            def body(b, first, last):
                if not last:
                    load_x(b + 1)
                    regroup(b + 1)
                spread_scores(b)
                if not last:
                    put_max(b + 1)
                if not first:
                    store(b - 1)

            pipeline(sp, body)
            store(B - 1)
            sp.wait_ge(out_d, 16 * B + 16)

        @block.gpsimd
        def _(pool):
            made = [0]

            def const(ins):
                made[0] += 1
                ins.then_inc(cst, 1)
                pool.wait_ge(cst, made[0])

            def keep(tile, pattern, base, cm, op=ALU.is_ge, val=NEG):
                const(nc.gpsimd.affine_select(out=tile, in_=tile, compare_op=op, fill=val, base=base,
                                              pattern=pattern, channel_multiplier=cm))

            def inverse(b, s, ln):
                pool.wait_ge(s["ve"], b + 1)
                nc.gpsimd.tensor_tensor(ln["rstd"][:], ln["ve"][:], mhalf[:].to_broadcast([128, NQB]),
                                        ALU.pow).then_inc(s["rstd"], 1)

            def gate_wo(b, first):
                if first:
                    pool.wait_ge(s_ma, 16)
                    pool.wait_ge(s_wom, 16 * H)
                else:
                    pool.wait_ge(wo_mm, 2 * b)
                nc.gpsimd.tensor_tensor(womg[:], wom[:], mall[:, bass.ds(b, 1), 0, :].to_broadcast([128, HJ, D]),
                                        ALU.mult).then_inc(wg_d, 1)

            def add_bias(b, first):
                if first:
                    pool.wait_ge(s_ma, 16)
                    pool.wait_ge(x_in, 16)
                else:
                    pool.wait_ge(x2_d, 2 * b)
                    pool.wait_ge(x_in, 16 * b + 16)
                nc.gpsimd.tensor_tensor(xb[:], xt[:], mall[:, bass.ds(b, 1), 2, :].to_broadcast([128, NQB, D]),
                                        ALU.add).then_inc(xb_d, 1)

            def low_h1(b):
                pool.wait_ge(l1["hh"], b + 1)
                nc.gpsimd.tensor_tensor(hlp[:, WIN:WIN + S], ln1["h"][:], hhp[:, WIN:WIN + S].bitcast(F32),
                                        ALU.subtract).then_inc(l1["hl"], 1)

            def low_h2(b):
                pool.wait_ge(l2["hh"], b + 1)
                nc.gpsimd.tensor_tensor(h2l[:], ln2["h"][:], h2h[:].bitcast(F32), ALU.subtract).then_inc(l2["hl"], 1)

            def finish(b):
                pool.wait_ge(f_d, b + 1)
                nc.gpsimd.tensor_tensor(yt[:], yt[:], x2c[:], ALU.add).then_inc(fin_d, 1)

            def keep_x2(b, first):
                pool.wait_ge(x2_d, 2 * b + 2)
                if not first:
                    pool.wait_ge(fin_d, b)
                nc.gpsimd.tensor_tensor(x2c[:].rearrange("p a d -> p (a d)"), x2[:].rearrange("p a d -> p (a d)"),
                                        zero[:].to_broadcast([128, S]), ALU.add).then_inc(x2c_d, 1)

            def expert(b, n, first):
                pool.wait_ge(u_d, NX * b + n + 1)
                nc.gpsimd.tensor_tensor(u[:, n % 2], t[:, n % 2], u[:, n % 2], ALU.mult).then_inc(w_d, 1)

            nc.gpsimd.memset(mhalf[:], -0.5).then_inc(out_d, 16)
            const(nc.gpsimd.memset(ident[:], 0.0))
            keep(ident[:], [[-1, 128]], 0, 1, ALU.not_equal, 1.0)
            const(nc.gpsimd.tensor_copy(identb[:], ident[:]))
            assert made[0] == IDENT
            const(nc.gpsimd.memset(g[:, 0], 1.0))
            const(nc.gpsimd.memset(g[:, 1], 0.0))
            assert made[0] == PLANES
            const(nc.gpsimd.memset(mq[:], 0.0))
            for j in range(HJ):
                rows = mq[MB * j:MB * j + MB]
                keep(rows, [[0, 3], [1, MK]], 0, -1)
                keep(rows, [[0, 3], [-1, MK]], 2 * WIN, 1)
            keep(mq[:, 0, :], [[1, MK]], -WIN, 0)
            keep(mq[:, 2, :], [[-1, MK]], MK - WIN - 1, 0)
            assert made[0] == MASKS
            inverse(0, l1, ln1)
            const(nc.gpsimd.memset(mk[:], 0.0))
            const(nc.gpsimd.memset(cap[:], -NEG))
            const(nc.gpsimd.memset(dsel[:], 0.0))
            const(nc.gpsimd.iota(iota8[:], [[1, NE]], base=0, channel_multiplier=0,
                                 allow_small_or_imprecise_dtypes=True))
            low_h1(0)
            for r in range(32 // NPB):
                keep(dsel[:, :, NPB * r:NPB * r + NPB], [[1, NPB], [-1, NPB]], 0, 0, ALU.not_equal, 1.0)
            const(nc.gpsimd.memset(rsel[:].bitcast(F32), 0.0))
            for row in (0, NPB):
                keep(rsel[:].rearrange("p k (c r) -> p k c r", c=HG), [[-1, NPB], [-32, HG], [0, 32]], -row, 1,
                     ALU.not_equal, 1.0)
            const(nc.gpsimd.memset(lowrow[:], -1.0))
            for c in range(HG):
                const(nc.gpsimd.memset(lowrow[32 * c:32 * c + NPB], 0.0))
            for tile, val in ((mk, NEG), (cap, 0.0)):
                keep(tile[:], [[0, 3], [-1, PB]], 0, 1, val=val)
                keep(tile[:], [[0, 3], [1, PB]], 2 * WIN, -1, val=val)
                keep(tile[:, 0, :], [[0, PB]], -WIN, 1, val=val)
                keep(tile[:, 2, :], [[0, PB]], 128 - WIN - 1, -1, val=val)
            nc.gpsimd.memset(zero[:], 0.0).then_inc(cst_all, 1)
            gate_wo(0, True)
            add_bias(0, True)

            def body(b, first, last):
                fill(expert, b, "maxima", first)
                if not last:
                    inverse(b + 1, l1, ln1)
                    low_h1(b + 1)
                fill(expert, b, "sums", first)
                fill(expert, b, "division", first)
                inverse(b, l2, ln2)
                if not last:
                    add_bias(b + 1, False)
                fill(expert, b, "norm", first)
                fill(expert, b, "features", first)
                if not last:
                    gate_wo(b + 1, False)
                low_h2(b)
                fill(expert, b, "router", first)
                expert(b, 0, first)
                if not first:
                    finish(b - 1)
                keep_x2(b, first)
                expert(b, 1, first)

            pipeline(pool, body)
            for n in range(CSPLIT, NX):
                expert(B - 1, n, False)
            finish(B - 1)

        @block.scalar
        def _(act):
            act.wait_ge(w_in, 112)
            nc.scalar.activation(cth[:], ct[:], ACT.Tanh, scale=0.5).then_inc(s_th, 1)
            nc.scalar.activation(wqh[:, 0], wqf[:, 0], ACT.Copy, scale=SCALE)
            nc.scalar.activation(wqh[:, 1:3], wqf[:, 1:3], ACT.Copy).then_inc(s_wh, 1)

            def modulate(b, s, ln, k, first):
                act.wait_ge(s["tr"], b + 1)
                if first:
                    act.wait_ge(s_md, 1)
                else:
                    act.wait_ge(s["hl"], b)
                nc.scalar.activation(ln["h"][:], ps["M1"][:], ACT.Identity, bias=col(mod, k, b),
                                     scale=col(mod, k + 1, b)).then_inc(s["h"], 1)

            def high_h1(b, first):
                act.wait_ge(l1["h"], b + 1)
                if not first:
                    act.wait_ge(v_mm, 2 * b)
                nc.scalar.activation(hhp[:, WIN:WIN + S], ln1["h"][:], ACT.Copy).then_inc(l1["hh"], 1)

            def high_qk(b, first):
                act.wait_ge(q_mm, b + 1)
                if first:
                    act.wait_ge(s_bq, 1)
                else:
                    act.wait_ge(q_scr_w, 48 * b)
                nc.scalar.activation(qh[:].rearrange("p (q n) -> p n q", n=NMB),
                                     ps["S0"][:].rearrange("p (n q) -> p n q", n=NMB),
                                     ACT.Identity, bias=bqs[:]).then_inc(q_h, 1)
                act.wait_ge(k_mm, b + 1)
                if not first:
                    act.wait_ge(k_scr_w, 48 * b)
                nc.scalar.activation(kh[:], ps["S1"][:], ACT.Identity, bias=bia[:, 1:2]).then_inc(k_h, 1)

            def copy_vf(b):
                act.wait_ge(vf_mm, b + 1)
                nc.scalar.activation(vf[:, WIN:WIN + S], ps["PV"][:], ACT.Copy).then_inc(vf_d, 1)

            def copy_v(b, first):
                if not first:
                    act.wait_ge(pv_mm, NPB * b)
                for half, bank in ((0, "PV"), (1, "M0")):
                    act.wait_ge(v_mm, 2 * b + half + 1)
                    nc.scalar.activation(v[:, 4 * half:4 * half + 4, :], ps[bank][:], ACT.Copy).then_inc(v_ev, 1)

            def maxima(b, first):
                act.wait_ge(mx_rd, NMB * b + NMB)
                if not first:
                    act.wait_ge(m_in, 64 * b)
                nc.scalar.activation(mn[:], mx[:], ACT.Copy, scale=-1.0).then_inc(mn_d, 1)

            def sums(b, i):
                act.wait_ge(pv_mm, NPB * b + 2 * i + 2)
                if i == 0 and not (isinstance(b, int) and b == 0):
                    act.wait_ge(wo_mm, 2 * b)
                nc.scalar.activation(pair_of_blocks(i), pv_ps[i % 2][:].rearrange("p (k j q) -> p k j q", k=2, j=HJ),
                                     ACT.Copy).then_inc(nm_d, 1)

            def high_rden(b):
                act.wait_ge(rden_d, b + 1)
                nc.scalar.activation(rdh[:], rden[:], ACT.Copy).then_inc(rdh_d, 1)

            def probabilities(b):
                for n in range(NSC):
                    blk, half = n // 2, n % 2
                    act.wait_ge(sc_mm, NSC * b + n + 1)
                    if blk >= NP:
                        act.wait_ge(pv_mm, NPB * b + blk - NP + 1)
                    nc.scalar.activation(p[:, blk % NP, 512 * half:512 * half + 512], sc_ps[n % 2][:],
                                         ACT.Exp).then_inc(exp_d, 1)
                    if n % 4 == 1 and n >= 9:
                        sums(b, n // 4 - 2)
                sums(b, NPB // 2 - 2)

            def high_h2(b, first):
                act.wait_ge(l2["h"], b + 1)
                if not first:
                    act.wait_ge(b_mm, NX * b)
                nc.scalar.activation(h2h[:], ln2["h"][:], ACT.Copy).then_inc(l2["hh"], 1)

            def router_exp(b):
                act.wait_ge(g_dl, b + 1)
                nc.scalar.activation(ex[:], dl[:], ACT.Exp).then_inc(g_ex, 1)

            def router_scores(b, first):
                act.wait_ge(smt_mm, b + 1)
                if not first:
                    act.wait_ge(s_wr, 16 * b)
                nc.scalar.activation(smT[:], ps["M1"][0:NQB * NE, 0:QB], ACT.Copy).then_inc(smt_cp, 1)

            def expert(b, n, first):
                if n == 0:
                    act.wait_ge(a_mm, NX * b + 1)
                    if not first:
                        act.wait_ge(w_d, NX * b)
                        act.wait_ge(g_d, NX * b)
                    nc.scalar.activation(t[:, 0], ps["A"][:], ACT.Copy).then_inc(t_d, 1)
                    act.wait_ge(b_mm, NX * b + 1)
                    nc.scalar.activation(u[:, 0], ps["B"][:], ACT.Copy).then_inc(u_d, 1)
                act.wait_ge(t_d, NX * b + n + 1)
                if n >= 2 or not first:
                    act.wait_ge(g_d, NX * b + max(n - 1, 0))
                nc.scalar.activation(th[:, n % 2], t[:, n % 2], ACT.Tanh, scale=0.5).then_inc(th_d, 1)

            modulate(0, l1, ln1, 0, True)
            high_h1(0, True)
            act.wait_ge(e_in, 32)
            nc.scalar.activation(w13h[:], w13f, ACT.Copy).then_inc(s_wh, 1)
            high_qk(0, True)
            copy_vf(0)
            copy_v(0, True)
            nc.scalar.activation(w2s[:], w2f, ACT.Copy, scale=0.5).then_inc(s_w2, 1)

            maxima(0, True)

            def body(b, first, last):
                fill(expert, b, "maxima", first)
                probabilities(b)
                sums(b, NPB // 2 - 1)
                if not last:
                    modulate(b + 1, l1, ln1, 0, False)
                high_rden(b)
                if not last:
                    high_h1(b + 1, False)
                fill(expert, b, "sums", first)
                fill(expert, b, "division", first)
                if not last:
                    high_qk(b + 1, False)
                    copy_vf(b + 1)
                fill(expert, b, "norm", first)
                modulate(b, l2, ln2, 2, first)
                if not last:
                    copy_v(b + 1, False)
                fill(expert, b, "features", first)
                router_exp(b)
                high_h2(b, first)
                router_scores(b, first)
                fill(expert, b, "router", first)
                expert(b, 0, first)
                if not last:
                    maxima(b + 1, False)
                expert(b, 1, first)

            pipeline(act, body)
            for n in range(CSPLIT, NX):
                expert(B - 1, n, False)

        @block.vector
        def _(dve):
            nc.vector.memset(wom[:], 0.0).then_inc(z_in, 1)
            for pad in (slice(0, WIN), slice(WIN + S, WIN + S + WIN)):
                nc.vector.memset(k4[:, :, pad].bitcast(F32), 0.0)
                nc.vector.memset(hhp[:, pad].bitcast(F32), 0.0)
                nc.vector.memset(vf[:, pad], 0.0)
                last = nc.vector.memset(hlp[:, pad].bitcast(F32), 0.0)
            last.then_inc(z_in, 1)
            nc.vector.memset(q4[:, 0:2].bitcast(F32), 0.0)
            dve.wait_ge(s_th, 1)
            nc.vector.scalar_tensor_tensor(cth[:], cth[:], 1.0, ct[:], ALU.add, ALU.mult).then_inc(s_sv, 1)
            dve.wait_ge(s_sv, 1)
            nc.vector.tensor_scalar(csl[:], cth[:], 0.5, None, ALU.mult).then_inc(s_sl, 1)
            dve.wait_ge(s_wh, 1)
            nc.vector.scalar_tensor_tensor(wql[:, 0], wqf[:, 0], SCALE, wqh[:, 0].bitcast(F32), ALU.mult, ALU.subtract)
            nc.vector.tensor_scalar(bqs[:], bia[:, 0:1], SCALE, None, ALU.mult).then_inc(s_bq, 1)
            nc.vector.tensor_tensor(wql[:, 1:3], wqf[:, 1:3], wqh[:, 1:3].bitcast(F32), ALU.subtract).then_inc(s_wl, 1)
            dve.wait_ge(s_mod, 1)
            pm = ps["M1"][:, 0:4 * B].rearrange("p (k b) -> p k b", k=4)
            nc.vector.tensor_copy(mod[:, 0:4:2], pm[:, 0:4:2])
            nc.vector.tensor_scalar(mod[:, 1:4:2], pm[:, 1:4:2], 1.0, None, ALU.add).then_inc(s_md, 1)

            def statistics(b, s, ln, src):
                for a in range(NQB):
                    last = nc.vector.bn_stats(ln["st"][:, a], src[:, a])
                last.then_inc(s["bn"], 1)

            def moments(b, s, ln):
                dve.wait_ge(s["bn"], 2 * b + 1)
                nc.vector.memset(spare[:], 0.0)
                for a in range(NQB):
                    last = nc.vector.bn_aggr(ln["mv"][:, a], ln["st"][:, a])
                last.then_inc(s["bn"], 1)
                dve.wait_ge(s["bn"], 2 * b + 2)
                nc.vector.tensor_scalar(ln["ve"][:], ln["mv"][:, :, 1], EPS, None, ALU.add).then_inc(s["ve"], 1)

            def normal(b, s, ln, src, first):
                dve.wait_ge(s["rstd"], b + 1)
                if not first:
                    dve.wait_ge(s["tr"], b)
                for a in range(NQB):
                    nc.vector.tensor_scalar(ln["xn"][:, a], src[:, a], ln["mv"][:, a, 0:1],
                                            ln["rstd"][:, a:a + 1], ALU.subtract, ALU.mult).then_inc(s["xn"], 1)

            def low_qk(b, first):
                dve.wait_ge(q_h, b + 1)
                if first:
                    dve.wait_ge(s_bq, 1)
                else:
                    dve.wait_ge(q_scr_w, 48 * b)
                nc.vector.scalar_tensor_tensor(ql[:].rearrange("p (q n) -> p n q", n=NMB),
                                               ps["S0"][:].rearrange("p (n q) -> p n q", n=NMB), bqs[:],
                                               qh[:].bitcast(F32).rearrange("p (q n) -> p n q", n=NMB),
                                               ALU.add, ALU.subtract).then_inc(q_l, 1)
                dve.wait_ge(k_h, b + 1)
                if not first:
                    dve.wait_ge(k_scr_w, 48 * b)
                nc.vector.scalar_tensor_tensor(kl[:], ps["S1"][:], bia[:, 1:2], kh[:].bitcast(F32),
                                               ALU.add, ALU.subtract).then_inc(k_l, 1)

            def maxima(b, first, lo, hi):
                if not first and lo == 0:
                    dve.wait_ge(mn_d, b)
                for n in range(lo, hi):
                    dve.wait_ge(ms_mm, NMB * b + n + 1)
                    nc.vector.tensor_reduce(mx[:, :, n], mx_ps[n % 4][:, 0:HG * MK].rearrange("p (g k) -> p g k", g=HG),
                                            AX.X, ALU.max).then_inc(mx_rd, 1)

            def mask(b, lo, hi):
                for blk in range(lo, hi):
                    edge = 0 if blk == 0 else 2 if blk == NPB - 1 else 1
                    for half in range(2):
                        if half == 0 and blk in PE_MASKS:
                            continue
                        dve.wait_ge(exp_d, NSC * b + 2 * blk + half + 1)
                        part = p[:, blk % NP, 512 * half:512 * half + 512].rearrange("p (k q) -> p k q", k=8)
                        nc.vector.tensor_tensor(part, part, cap[:, edge, :].unsqueeze(1).to_broadcast([128, 8, PB]),
                                                ALU.min).then_inc(p_d, 1)

            def invert_sums(b):
                dve.wait_ge(pv_mm, NPB * b + NPB)
                nc.vector.reciprocal(rden[:], ps["M0"][:, 0:256]).then_inc(rden_d, 1)

            def halve_rden(b):
                dve.wait_ge(rdh_d, b + 1)
                nc.vector.scalar_tensor_tensor(rdx[:], rdh[:].bitcast(F32), lowrow[:], rden[:],
                                               ALU.mult, ALU.add).then_inc(rdx_d, 1)

            def normalise(b):
                dve.wait_ge(nm_d, NPB // 2 * b + NPB // 2)
                for i in range(NPB // 2):
                    dve.wait_ge(rb_mm, NPB // 2 * b + i + 1)
                    nc.vector.tensor_tensor(pair_of_blocks(i), pair_of_blocks(i),
                                            rb_ps[i][:].rearrange("p (k j q) -> p k j q", k=2, j=HJ),
                                            ALU.mult).then_inc(o_d, 1)

            def residual(b, first):
                dve.wait_ge(xb_d, b + 1)
                if not first:
                    dve.wait_ge(x2c_d, b)
                for half, bank in ((0, "M1"), (1, "M0")):
                    a = slice(2 * half, 2 * half + 2)
                    dve.wait_ge(wo_mm, 2 * b + half + 1)
                    nc.vector.tensor_tensor(x2[:, a], ps[bank][:, 0:2 * D].rearrange("p (a d) -> p a d", a=2),
                                            xb[:, a], ALU.add).then_inc(x2_d, 1)
                    dve.wait_ge(x2_d, 2 * b + half + 1)
                    for a in range(2 * half, 2 * half + 2):
                        last = nc.vector.bn_stats(ln2["st"][:, a], x2[:, a])
                last.then_inc(l2["bn"], 1)

            def router(b, part):
                done = [part]

                def link(ins):
                    done[0] += 1
                    ins.then_inc(g_ch, 1)
                    dve.wait_ge(g_ch, NG * b + done[0])

                lg = ps["M1"][:, 0:NQB * NE].rearrange("p (a e) -> p a e", a=NQB)
                bc = [128, NQB, NE]
                if part == 0:
                    dve.wait_ge(g_mm, b + 1)
                    link(nc.vector.tensor_reduce(rm[:], lg, AX.X, ALU.max))
                    nc.vector.tensor_tensor(dl[:], lg, rm[:].unsqueeze(2).to_broadcast(bc),
                                            ALU.subtract).then_inc(g_dl, 1)
                    return
                dve.wait_ge(g_ex, b + 1)
                link(nc.vector.tensor_reduce(es[:], ex[:], AX.X, ALU.add))
                link(nc.vector.reciprocal(er[:], es[:]))
                link(nc.vector.tensor_tensor(sc[:], ex[:], er[:].unsqueeze(2).to_broadcast(bc), ALU.mult))
                nc.vector.memset(spare[:], 0.0)
                for a in range(NQB):
                    last = nc.vector.max(m8[:, a, :], sc[:, a, :])
                link(last)
                nc.vector.memset(spare[:], 0.0)
                for a in range(NQB):
                    last = nc.vector.max_index(ix[:, a, :], m8[:, a, :], sc[:, a, :])
                link(last)
                link(nc.vector.tensor_copy(ixf[:], ix[:, :, 0:2]))
                for r in range(2):
                    link(nc.vector.tensor_tensor(sel[:, r], iota8[:].unsqueeze(1).to_broadcast(bc),
                                                 ixf[:, :, r:r + 1].to_broadcast(bc), ALU.is_equal))
                link(nc.vector.tensor_tensor(selb[:], sel[:, 0], sel[:, 1], ALU.add))
                nc.vector.tensor_tensor(sm[:].rearrange("p e a -> p a e"), sc[:], selb[:], ALU.mult).then_inc(g_ch, 1)
                assert done[0] + 1 == NG

            def gate_w(n, dst, bank):
                return nc.vector.tensor_tensor(dst[:, n % 2], bank[:], sbc[:, n - 1], ALU.mult)

            def combine(b, n, first):
                dve.wait_ge(th_d, NX * b + n + 1)
                dve.wait_ge(w_d, NX * b + n + 1)
                if n >= 2 or not first:
                    dve.wait_ge(y_mm, NX * b + max(n - 1, 0))
                nc.vector.scalar_tensor_tensor(g[:, n % 2], th[:, n % 2], 1.0, u[:, n % 2],
                                               ALU.add, ALU.mult).then_inc(g_d, 1)

            def expert(b, n, first):
                if n >= 1:
                    dve.wait_ge(a_mm, NX * b + n + 1)
                    if n % 2 == 1:
                        dve.wait_ge(s_in[n // 2], 16 * b + 16)
                    if n >= 2 or not first:
                        dve.wait_ge(w_d, NX * b + n - 1)
                        dve.wait_ge(th_d, NX * b + n - 1)
                    gate_w(n, t, ab_ps[n][0]).then_inc(t_d, 1)
                    if n >= 2 or not first:
                        dve.wait_ge(g_d, NX * b + n - 1)
                    dve.wait_ge(b_mm, NX * b + n + 1)
                    gate_w(n, u, ab_ps[n][1]).then_inc(u_d, 1)
                    if n in (2, 3, 5, 6, 7):
                        combine(b, n - 1, first)

            def finish(b):
                dve.wait_ge(y_mm, NX * b + NX)
                dve.wait_ge(out_d, 16 * b + 16)
                nc.vector.tensor_tensor(yt[:], ps["Y"][:].rearrange("p (a d) -> p a d", a=NQB),
                                        mall[:, bass.ds(b, 1), 1, :].to_broadcast([128, NQB, D]),
                                        ALU.mult).then_inc(f_d, 1)

            def split_experts():
                dve.wait_ge(s_wh, 2)
                nc.vector.tensor_tensor(w13l[:], w13f, w13h[:].bitcast(F32), ALU.subtract).then_inc(s_wl, 1)

            dve.wait_ge(x_in, 16)
            statistics(0, l1, ln1, xt)
            moments(0, l1, ln1)
            normal(0, l1, ln1, xt, True)
            nc.vector.memset(q4[:, 2:4].bitcast(F32), 0.0).then_inc(z_in, 1)
            low_qk(0, True)
            split_experts()
            dve.wait_ge(s_bo, 1)
            nc.vector.tensor_copy(mraw, ps["Y"][0:B, 0:2 * D]).then_inc(s_sv, 1)
            nc.vector.tensor_tensor(bo2, ps["Y"][0:B, 2 * D:3 * D], bob, ALU.add).then_inc(s_sv, 1)
            dve.wait_ge(s_sv, 3)
            nc.vector.tensor_scalar(mneg, mraw, -1.0, None, ALU.mult).then_inc(s_sv, 1)
            nc.vector.tensor_scalar(msgn, mraw, 0.0, 2.0, ALU.is_ge, ALU.mult).then_inc(s_sv, 1)
            dve.wait_ge(s_sv, 5)
            nc.vector.tensor_tensor(mabs, mneg, mraw, ALU.max).then_inc(s_sv, 1)
            dve.wait_ge(s_sv, 6)
            nc.vector.tensor_scalar(mneg, mabs, 0.25, None, ALU.max).then_inc(s_sv, 1)
            dve.wait_ge(s_sv, 7)
            nc.vector.scalar_tensor_tensor(mrow[:, 0:2], msgn, -1.0, mneg, ALU.add, ALU.mult).then_inc(s_sv, 1)
            dve.wait_ge(s_sv, 8)
            nc.vector.tensor_tensor(mrow[:, 2], mrow[:, 0], bo2, ALU.mult).then_inc(s_mr, 1)

            maxima(0, True, 0, NMB)

            def body(b, first, last):
                fill(expert, b, "maxima", first)
                mask(b, 0, 2)
                if not first:
                    combine(b - 1, 3, False)
                if not last:
                    dve.wait_ge(x_in, 16 * b + 32)
                    statistics(b + 1, l1, ln1, xt)
                mask(b, 2, 3)
                if not last:
                    moments(b + 1, l1, ln1)
                mask(b, 3, 5)
                if not last:
                    normal(b + 1, l1, ln1, xt, False)
                mask(b, 5, NPB)
                invert_sums(b)
                halve_rden(b)
                fill(expert, b, "sums", first)
                normalise(b)
                fill(expert, b, "division", first)
                if not last:
                    low_qk(b + 1, False)
                residual(b, first)
                moments(b, l2, ln2)
                normal(b, l2, ln2, x2, first)
                fill(expert, b, "norm", first)
                fill(expert, b, "features", first)
                router(b, 0)
                router(b, 1)
                if not last:
                    maxima(b + 1, False, 0, 6)
                fill(expert, b, "router", first)
                if not first:
                    combine(b - 1, NX - 2, False)
                if not last:
                    maxima(b + 1, False, 6, 8)
                if not first:
                    combine(b - 1, NX - 1, False)
                if not last:
                    maxima(b + 1, False, 8, 12)
                if not first:
                    finish(b - 1)
                if not last:
                    maxima(b + 1, False, 12, NMB)
                combine(b, 0, first)
                expert(b, 1, first)

            pipeline(dve, body)
            for n in range(CSPLIT, NX):
                expert(B - 1, n, False)
                if n == 4:
                    combine(B - 1, 3, False)
            combine(B - 1, NX - 2, False)
            combine(B - 1, NX - 1, False)
            finish(B - 1)

        @block.tensor
        def _(pe):
            mm = nc.tensor.matmul

            heads = q4[:].rearrange("p g j s -> p g (j s)")
            queries = q4[:].rearrange("p g j (q n) -> p g j q n", n=NMB)

            def exact3(dst, wh, wl, xh, xl):
                mm(dst, wh, xh, start=True, stop=False)
                mm(dst, wl, xh, start=False, stop=False)
                return mm(dst, wh, xl, start=False, stop=True)

            pe.wait_ge(w_in, 112)
            pe.wait_ge(s_sl, 1)
            for i, k in enumerate((0, 1, 3, 4)):
                last = mm(ps["M1"][:, i * B:i * B + B], wm[:, k, :], csl[:], start=True, stop=True)
            last.then_inc(s_mod, 1)
            for i, k in enumerate((2, 5)):
                mm(ps["Y"][0:B, i * D:i * D + D], csl[:], wm[:, k, :], start=True, stop=True)
            mm(ps["Y"][0:B, 2 * D:3 * D], bia[:, 2:3].to_broadcast([128, B]), wof, start=True, stop=True)\
                .then_inc(s_bo, 1)

            def flip(b, s, ln, bank):
                for a in range(NQB):
                    pe.wait_ge(s["xn"], NQB * b + a + 1)
                    last = nc.tensor.transpose(ps[bank][:, QB * a:QB * a + QB], ln["xn"][:, a], ident[:])
                last.then_inc(s["tr"], 1)

            def project_qk(b, first):
                pe.wait_ge(l1["hl"], b + 1)
                hh, hl = hhp[:, WIN:WIN + S], hlp[:, WIN:WIN + S]
                if not first:
                    pe.wait_ge(o_d, NPB // 2 * b - 3)
                exact3(ps["S0"][:], wqh[:, 0, :], wql[:, 0, :], hh, hl).then_inc(q_mm, 1)
                if not first:
                    pe.wait_ge(o_d, NPB // 2 * b - 2)
                exact3(ps["S1"][:], wqh[:, 1, :], wql[:, 1, :], hh, hl).then_inc(k_mm, 1)

            def project_v(b):
                exact3(ps["PV"][:], wqh[:, 2, :], wql[:, 2, :], hhp[:, WIN:WIN + S],
                       hlp[:, WIN:WIN + S]).then_inc(vf_mm, 1)

            def flip_v(b):
                pe.wait_ge(vf_d, b + 1)
                if not (isinstance(b, int) and b == 0):
                    pe.wait_ge(x2_d, 2 * b)
                for half, bank in ((0, "PV"), (1, "M0")):
                    for i in range(4):
                        start = PB * (4 * half + i)
                        last = nc.tensor.transpose(ps[bank][:, 128 * i:128 * i + 128],
                                                   vf[:, start:start + 128], ident[:])
                    last.then_inc(v_mm, 1)

            def maxima(b, lo, hi):
                if lo == 0:
                    pe.wait_ge(qk_in, 96 * b + 96)
                for n in range(lo, hi):
                    edge = 0 if n == 0 else 2 if n == NMB - 1 else 1
                    if n == 0:
                        pe.wait_ge(v_ev, 2 * b + 2)
                    if n == 2 and not (isinstance(b, int) and b <= 1):
                        pe.wait_ge(u_d, NX * b - NX - 1)
                    if n >= 4:
                        pe.wait_ge(mx_rd, NMB * b + n - 3)
                    bank = mx_ps[n % 4]
                    mm(bank[:, 0:HG * MK], identb[:], mq[:, edge, :].unsqueeze(1).to_broadcast([128, HG, MK]),
                       start=True, stop=False)
                    for gg in range(HG):
                        last = mm(bank[:, MK * gg:MK * gg + MK], heads[:, gg, n:NMB * (HJ * MB - 1) + n + 1:NMB],
                                  k4[:, gg, MB * n:MB * n + MK], start=False, stop=gg == HG - 1)
                    last.then_inc(ms_mm, 1)

            def values(b, blk):
                if blk in PE_MASKS:
                    pe.wait_ge(exp_d, NSC * b + 2 * blk + 1)
                pe.wait_ge(p_d, (NSC - len(PE_MASKS)) * b + 2 * blk + 2 - len([m for m in PE_MASKS if m <= blk]))
                if blk == 0:
                    pe.wait_ge(v_ev, 2 * b + 2)
                elif blk % 2 == 0 and blk >= 4:
                    pe.wait_ge(nm_d, NPB // 2 * b + blk // 2 - 1)
                for c in range(HG):
                    r = slice(32 * c, 32 * c + 32)
                    mm(pv_ps[blk // 2 % 2][r, 256 * (blk % 2):256 * (blk % 2) + 256], v[:, blk, r],
                       p[:, blk % NP, 256 * c:256 * c + 256], start=True, stop=True)
                for c in range(HG):
                    r = slice(32 * c, 32 * c + 32)
                    last = mm(ps["M0"][r, 0:256], dsel[:, blk, :], p[:, blk % NP, 256 * c:256 * c + 256],
                              start=blk == 0, stop=blk == NPB - 1)
                last.then_inc(pv_mm, 1)

            def scores(b, first, final):
                pe.wait_ge(m_in, 64 * b + 64)
                if not first:
                    pe.wait_ge(smt_cp, b)
                for blk in range(NPB):
                    edge = 0 if blk == 0 else 2 if blk == NPB - 1 else 1
                    for half in range(2):
                        n = 2 * blk + half
                        if n >= 2:
                            pe.wait_ge(exp_d, NSC * b + n - 1)
                        bank = sc_ps[n % 2]
                        masked = half == 0 and blk in PE_MASKS
                        if masked:
                            mm(bank[:], identb[:], mk[:, edge, :].unsqueeze(1).to_broadcast([128, 8, PB]),
                               start=True, stop=False)
                        for a in range(2):
                            gg = 2 * half + a
                            done = mm(bank[:, 256 * a:256 * a + 256], k4[:, gg, PB * blk:PB * blk + 128],
                                      queries[:, gg, :, :, 2 * blk:2 * blk + 2].rearrange("p j q n -> p j n q"),
                                      start=not masked, stop=not masked or a == 1)
                        done.then_inc(sc_mm, 1)
                    if blk < 2 and not first:
                        down(b - 1, blk + 1, False)
                    if blk >= 2:
                        values(b, blk - 2)
                values(b, NPB - 2)
                values(b, NPB - 1)
                if not final:
                    pe.wait_ge(nm_d, NPB // 2 * b + NPB // 2 - 1)
                    flip(b + 1, l1, ln1, "M1")

            def spread_rden(b):
                pe.wait_ge(rdx_d, b + 1)
                pe.wait_ge(nm_d, NPB // 2 * b + NPB // 2)
                for i in range(NPB // 2):
                    for k in range(2):
                        dst = rb_ps[i][:, 256 * k:256 * k + 256]
                        last = mm(dst, rsel[:, 2 * i + k, :], rdx[:], start=True, stop=True)
                    last.then_inc(rb_mm, 1)

            def attn_out(b):
                pe.wait_ge(wg_d, b + 1)
                pe.wait_ge(o_d, NPB // 2 * b + NPB // 2)
                for a in range(NQB):
                    for j in range(HJ):
                        last = mm(ps["M1" if a < 2 else "M0"][:, D * (a % 2):D * (a % 2) + D],
                                  o[:, j, QB * a:QB * a + QB], womg[:, j, :], start=j == 0, stop=j == HJ - 1)
                    if a % 2 == 1:
                        last.then_inc(wo_mm, 1)

            def router(b):
                pe.wait_ge(l2["h"], b + 1)
                for a in range(NQB):
                    last = mm(ps["M1"][:, NE * a:NE * a + NE], ln2["h"][:, QB * a:QB * a + QB], gw[:],
                              start=True, stop=True)
                last.then_inc(g_mm, 1)

            def router_t(b):
                pe.wait_ge(g_ch, NG * b + NG)
                nc.tensor.transpose(ps["M1"][0:NQB * NE, 0:QB], sm[:].rearrange("p e a -> p (e a)"),
                                    ident[:]).then_inc(smt_mm, 1)

            def down(b, n, first):
                pe.wait_ge(g_d, NX * b + n + 1)
                if n == 0 and not first:
                    pe.wait_ge(f_d, b)
                e = (n - 1) % NX
                for a in range(NQB):
                    last = mm(ps["Y"][:, QB * a:QB * a + QB], g[:, n % 2, QB * a:QB * a + QB], w2s[:, e, :],
                              start=n == 0 and a == 0, stop=n == NX - 1, skip_group_check=True)
                last.then_inc(y_mm, 1)

            def expert(b, n, first):
                e = (n - 1) % NX
                if n == 0:
                    pe.wait_ge(l2["hl"], b + 1)
                done = n - 1 if n - 1 in (2, 7) else n
                a_ps, b_ps = ab_ps[n]
                if n == 2:
                    if not (isinstance(b, int) and b == B - 1):
                        pe.wait_ge(mx_rd, NMB * b + 2 * NMB - 2)
                elif n != 7 and (done >= 1 or not first):
                    pe.wait_ge(t_d, NX * b + done)
                exact3(a_ps[:], w13h[:, e, 0, :], w13l[:, e, 0, :], h2h[:], h2l[:]).then_inc(a_mm, 1)
                if n not in (2, 7) and (done >= 1 or not first):
                    pe.wait_ge(u_d, NX * b + done)
                exact3(b_ps[:], w13h[:, e, 1, :], w13l[:, e, 1, :], h2h[:], h2l[:]).then_inc(b_mm, 1)
                if n >= 6:
                    down(b, n - 2, first)

            pe.wait_ge(s_md, 1)
            pe.wait_ge(cst, IDENT)
            flip(0, l1, ln1, "M1")
            pe.wait_ge(s_wl, 1)
            pe.wait_ge(z_in, 2)
            project_qk(0, True)
            project_v(0)
            flip_v(0)

            pe.wait_ge(cst, MASKS)
            maxima(0, 0, NMB)
            pe.wait_ge(cst_all, 1)

            def body(b, first, last):
                fill(expert, b, "maxima", first)
                scores(b, first, last)
                fill(expert, b, "sums", first)
                if not first:
                    down(b - 1, 3, False)
                spread_rden(b)
                fill(expert, b, "division", first)
                if not last:
                    project_qk(b + 1, False)
                attn_out(b)
                if not last:
                    project_v(b + 1)
                fill(expert, b, "norm", first)
                if not last:
                    flip_v(b + 1)
                flip(b, l2, ln2, "M1")
                fill(expert, b, "features", first)
                router(b)
                fill(expert, b, "router", first)
                if not last:
                    maxima(b + 1, 0, 4)
                router_t(b)
                if first:
                    pe.wait_ge(s_wl, 2)
                    pe.wait_ge(s_w2, 1)
                if not last:
                    maxima(b + 1, 4, 10)
                if not first:
                    down(b - 1, NX - 2, False)
                if not last:
                    maxima(b + 1, 10, 12)
                if not first:
                    down(b - 1, NX - 1, False)
                expert(b, 0, first)
                if not last:
                    maxima(b + 1, 12, NMB)
                expert(b, 1, first)
                down(b, 0, first)

            pipeline(pe, body)
            for n in range(CSPLIT, NX):
                expert(B - 1, n, False)
                if n in (3, 4, 5):
                    down(B - 1, n - 2, False)
            down(B - 1, NX - 2, False)
            down(B - 1, NX - 1, False)


def kernel(**inputs):
    import concourse.bacc as bacc
    from concourse.bass_utils import run_bass_kernel_spmd

    a = {k: np.asarray(x) for k, x in inputs.items()}
    order = np.arange(D).reshape(HG, HJ, DH).transpose(1, 2, 0).reshape(-1)
    lay = {
        "x": a["L0_attn_x"],
        "w13": np.stack([np.concatenate([a["L0_ffn_w1"], a["L0_ffn_w1s"]]),
                         np.concatenate([a["L0_ffn_w3"], a["L0_ffn_w3s"]])]).transpose(2, 1, 0, 3),
        "w2": np.concatenate([a["L0_ffn_w2"], a["L0_ffn_w2s"]]).transpose(1, 0, 2),
        "wqkv": np.stack([a["L0_attn_wq"][order], a["L0_attn_wk"][order], a["L0_attn_wv"]]).transpose(2, 0, 1),
        "wo": a["L0_attn_wo"].T,
        "gate": a["L0_ffn_gate_w"].T,
        "bias": np.stack([a["L0_attn_bq"][order], a["L0_attn_bk"][order], a["L0_attn_bv"], a["L0_attn_bo"]]).T,
        "borow": a["L0_attn_bo"][None],
        "cT": a["L0_c"].T,
        "wmod": a["L0_wmod"].reshape(D, 6, D),
    }
    nc = bacc.Bacc("TRN2", target_bir_lowering=False, num_devices=1)
    arrays, args = {}, []
    for name, x in lay.items():
        arrays[name] = np.ascontiguousarray(x)
        args.append(nc.dram_tensor(name, x.shape, F32, kind="ExternalInput").ap())
    args.append(nc.dram_tensor("out", (B, S, D), F32, kind="ExternalOutput").ap())
    build(nc, *args)
    r = run_bass_kernel_spmd(nc, [arrays], core_ids=[0])
    return r.results[0]["out"]
```
